# Optimizing a Trainium2 kernel written in Bass

```python
import numpy as np
import jax
import jax.numpy as jnp

def _softmax(x, axis=-1):
    return jax.nn.softmax(x, axis=axis)

def _gelu(x):
    return jax.nn.gelu(x, approximate=True)

def _silu(x):
    return jax.nn.silu(x)

def _sigmoid(x):
    return jax.nn.sigmoid(x)

def _layernorm(x, axis=-1, eps=1e-05):
    m = jnp.mean(x, axis=axis, keepdims=True)
    v = jnp.var(x, axis=axis, keepdims=True)
    return (x - m) / jnp.sqrt(v + eps)

def _scatter_add(tgt, idx, src, axis=0):
    return tgt.at[idx].add(src)

def _segment_sum(src, seg, n):
    return jax.ops.segment_sum(src, seg, n)
kernel_name = 'mk_adaln_d1_jaxref_r8_f899e5'

def setup_inputs(seed: int=0):
    np.random.seed(seed)
    _w = jnp.asarray

    def _L0_attn_setup():
        import jax, jax.numpy as jnp
        import numpy as np
        FP32_EPS = 1.1920929e-07

        def rms_norm(x):
            return x * jax.lax.rsqrt(jnp.mean(x * x, axis=-1, keepdims=True) + FP32_EPS)
        key = jax.random.key(seed)
        k1, k2, k3, k4 = jax.random.split(key, 4)
        n_embd, n_qkv = (128, 128)
        B, T = (4, 1024)

        def casted_init(k, out_f, in_f):
            s = 3.0 ** 0.5 * in_f ** (-0.5)
            return jax.random.uniform(k, (out_f, in_f), jnp.float32, -s, s)
        return {'x': jax.random.normal(k1, (B, T, n_embd), jnp.float32), 'w_qkv': casted_init(k2, 3 * n_qkv, n_embd), 'w_swiglu': casted_init(k3, 2 * n_embd, n_qkv), 'w_out': casted_init(k4, n_embd, n_embd)}
    _L0_attn_in = _L0_attn_setup()

    def _L0_ffn_setup():
        import jax, jax.numpy as jnp
        import numpy as np
        import math
        D_MODEL = 128
        N_EXPERTS = 16
        D_FF = 512
        CAP_FACTOR = 1.25
        MIN_CAPACITY = 4

        def _capacity(num_tokens, num_experts):
            cap = math.floor(CAP_FACTOR * num_tokens / num_experts)
            cap += cap % 2
            return max(cap, MIN_CAPACITY)

        def _top1_router(gate_logits, capacity):
            s, e = gate_logits.shape
            probs = jax.nn.softmax(gate_logits, axis=-1)
            top1 = jnp.argmax(gate_logits, axis=-1)
            mask = jax.nn.one_hot(top1, e, dtype=jnp.int32)
            ranks = jnp.cumsum(mask, axis=0) - 1
            mask = mask * (ranks < capacity).astype(jnp.int32)
            rank1 = jnp.sum(mask * ranks, axis=-1)
            ranks_oh = jax.nn.one_hot(rank1, capacity, dtype=probs.dtype)
            weight = mask.astype(probs.dtype) * probs
            combine_weights = weight[:, :, None] * ranks_oh[:, None, :]
            sec_mask = combine_weights > 0
            return (combine_weights, sec_mask)
        key = jax.random.key(seed)
        k1, k2, k3, k4 = jax.random.split(key, 4)
        x = jax.random.normal(k1, (4, 256, D_MODEL), dtype=jnp.float32)
        gate_w = jax.random.normal(k2, (N_EXPERTS, D_MODEL), dtype=jnp.float32) * math.sqrt(0.1 / D_MODEL)
        w1 = jax.random.normal(k3, (N_EXPERTS, D_MODEL, D_FF), dtype=jnp.float32) * (1.0 / math.sqrt(D_MODEL))
        w2 = jax.random.normal(k4, (N_EXPERTS, D_FF, D_MODEL), dtype=jnp.float32) * (1.0 / math.sqrt(D_FF))
        return {'x': x, 'gate_w': gate_w, 'w1': w1, 'w2': w2}
    _L0_ffn_in = _L0_ffn_setup()
    _L0_c = _w((lambda *s: np.random.randn(*s).astype(np.float32) * 0.05)(8, 128))
    _L0_wmod = _w((lambda *s: np.random.randn(*s).astype(np.float32) * 0.05)(128, 6 * 128) * 128 ** (-0.5))
    _d = {'L0_attn_x': _L0_attn_in['x'], 'L0_attn_w_qkv': _L0_attn_in['w_qkv'], 'L0_attn_w_swiglu': _L0_attn_in['w_swiglu'], 'L0_attn_w_out': _L0_attn_in['w_out'], 'L0_ffn_gate_w': _L0_ffn_in['gate_w'], 'L0_ffn_w1': _L0_ffn_in['w1'], 'L0_ffn_w2': _L0_ffn_in['w2'], 'L0_c': _L0_c, 'L0_wmod': _L0_wmod}
    _x0 = _d['L0_attn_x']
    _d['L0_attn_x'] = jax.random.normal(jax.random.fold_in(jax.random.key(seed), 1), (8, 512, 128), dtype=_x0.dtype)
    del _x0
    return _d

def reference(L0_attn_x, L0_attn_w_qkv, L0_attn_w_swiglu, L0_attn_w_out, L0_ffn_gate_w, L0_ffn_w1, L0_ffn_w2, L0_c, L0_wmod):

    def _L0_attn_ref(x, w_qkv, w_swiglu, w_out):
        import jax, jax.numpy as jnp
        import numpy as np
        FP32_EPS = 1.1920929e-07

        def rms_norm(x):
            return x * jax.lax.rsqrt(jnp.mean(x * x, axis=-1, keepdims=True) + FP32_EPS)
        qkv = jnp.einsum('btd,ed->bte', rms_norm(x), w_qkv)
        q, k, v = jnp.split(qkv, 3, axis=-1)
        q = rms_norm(q)
        k = rms_norm(k)
        w = jnp.exp(k)
        kv = w * v
        w = jnp.cumsum(w, axis=1)
        kv = jnp.cumsum(kv, axis=1)
        y = kv / (w + 1e-06)
        y = jax.nn.sigmoid(q) * y
        uv = jnp.einsum('bte,fe->btf', y, w_swiglu)
        u, g = jnp.split(uv, 2, axis=-1)
        return x + jnp.einsum('btd,ed->bte', u * jax.nn.silu(g), w_out)

    def _L0_ffn_ref(x, gate_w, w1, w2):
        import jax, jax.numpy as jnp
        import numpy as np
        import math
        D_MODEL = 128
        N_EXPERTS = 16
        D_FF = 512
        CAP_FACTOR = 1.25
        MIN_CAPACITY = 4

        def _capacity(num_tokens, num_experts):
            cap = math.floor(CAP_FACTOR * num_tokens / num_experts)
            cap += cap % 2
            return max(cap, MIN_CAPACITY)

        def _top1_router(gate_logits, capacity):
            s, e = gate_logits.shape
            probs = jax.nn.softmax(gate_logits, axis=-1)
            top1 = jnp.argmax(gate_logits, axis=-1)
            mask = jax.nn.one_hot(top1, e, dtype=jnp.int32)
            ranks = jnp.cumsum(mask, axis=0) - 1
            mask = mask * (ranks < capacity).astype(jnp.int32)
            rank1 = jnp.sum(mask * ranks, axis=-1)
            ranks_oh = jax.nn.one_hot(rank1, capacity, dtype=probs.dtype)
            weight = mask.astype(probs.dtype) * probs
            combine_weights = weight[:, :, None] * ranks_oh[:, None, :]
            sec_mask = combine_weights > 0
            return (combine_weights, sec_mask)
        tokens = x.reshape(-1, D_MODEL)
        s = tokens.shape[0]
        capacity = _capacity(s, N_EXPERTS)
        gate_logits = tokens.astype(jnp.float32) @ gate_w.T
        combine_weights, sec_mask = _top1_router(gate_logits, capacity)
        dispatch = jnp.einsum('sec,sd->ecd', sec_mask.astype(tokens.dtype), tokens)
        h = jax.nn.gelu(jnp.einsum('ecd,edf->ecf', dispatch, w1))
        expert_out = jnp.einsum('ecf,efd->ecd', h, w2)
        out = jnp.einsum('sec,ecd->sd', combine_weights.astype(tokens.dtype), expert_out)
        return out.reshape(x.shape)
    x = L0_attn_x
    mod = (_silu(L0_c) @ L0_wmod).reshape(L0_c.shape[0], 6, 1, -1)
    sa, ca, ga, sb, cb, gb = (mod[:, 0], mod[:, 1], mod[:, 2], mod[:, 3], mod[:, 4], mod[:, 5])
    ga = (2 * (ga >= 0) - 1) * jnp.maximum(jnp.abs(ga), 0.25)
    gb = (2 * (gb >= 0) - 1) * jnp.maximum(jnp.abs(gb), 0.25)
    h = _layernorm(x, axis=-1) * (1 + ca) + sa
    x = x + ga * _L0_attn_ref(h, L0_attn_w_qkv, L0_attn_w_swiglu, L0_attn_w_out)
    h = _layernorm(x, axis=-1) * (1 + cb) + sb
    x = x + gb * _L0_ffn_ref(h, L0_ffn_gate_w, L0_ffn_w1, L0_ffn_w2)
    return x

_drawn_inputs = setup_inputs


def setup_inputs(seed=0):
    import zlib

    import numpy as np

    out = dict(_drawn_inputs(seed))
    spreads = {}
    factors = {'L0_attn_w_qkv': 8.0,
     'L0_attn_w_swiglu': 7.444,
     'L0_attn_w_out': 7.459,
     'L0_ffn_gate_w': 25.848,
     'L0_ffn_w1': 27.04,
     'L0_ffn_w2': 24.32}
    for name, (base, spread) in spreads.items():
        noise = np.random.default_rng([zlib.crc32(name.encode()), seed]).standard_normal(out[name].shape)
        drawn = base * np.exp(spread * noise) if base else spread * noise
        out[name] = jnp.asarray(drawn.astype(out[name].dtype))
    for name, factor in factors.items():
        out[name] = (out[name] * factor).astype(out[name].dtype)
    return out
```

```python
import concourse.bass as bass
from concourse import mybir
from contextlib import ExitStack


def adaln_attention_moe(
    nc: bass.Bass,
    x_d: bass.AP,
    w_qkv_d: bass.AP,
    w_swiglu_d: bass.AP,
    w_out_d: bass.AP,
    gate_w_d: bass.AP,
    w1_d: bass.AP,
    w2_d: bass.AP,
    c_d: bass.AP,
    wmod_d: bass.AP,
    out_d: bass.AP,
):
    f32 = mybir.dt.float32
    bf16 = mybir.dt.bfloat16
    i32 = mybir.dt.int32
    ALU = mybir.AluOpType
    ACT = mybir.ActivationFunctionType
    X = mybir.AxisListType.X

    P = 128
    NB, T, D = x_d.shape
    NJ = T // P
    NTOK = NB * T
    NE, _, FF = w1_d.shape
    NF = FF // P
    CAP = int(1.25 * NTOK / NE)
    CAP += CAP % 2
    NSLOT = NE * CAP
    NPAIR = NE // 2
    PS = 2 * CAP
    NS = PS // P
    EPS_RMS = 1.1920929e-07
    EPS_LN = 1e-05
    NOWHERE = 1 << 20
    C_X1, C_GP, C_TOK, ROW = D, 2 * D, 3 * D, 3 * D + 2
    SA, CA, GA, SB, CB, GB = range(6)

    disp_d = nc.dram_tensor("dispatched_rows", [NSLOT, ROW], f32, kind="Internal").ap()

    ctx = ExitStack()
    with ctx:
        def sb(name, shape, dt=f32):
            return ctx.enter_context(nc.sbuf_tensor(name, shape, dt))

        def sem(name):
            return ctx.enter_context(nc.semaphore(name))

        bank01 = ctx.enter_context(nc.psum_tensor("bank01", [P, 1024], f32))
        bank67 = ctx.enter_context(nc.psum_tensor("bank67", [P, 1024], f32))
        bank2, bank3, bank4, bank5 = [
            ctx.enter_context(nc.psum_tensor(f"bank{n}", [P, 512], f32)) for n in (2, 3, 4, 5)]
        ps_qk = bank01[:, :].rearrange("p (j c) -> p j c", j=NJ)
        ps_t = bank2[:, :]
        ps_v = bank3[:, :].rearrange("p (j c) -> p j c", j=NJ)
        ps_w = bank4[:, :]
        ps_kv = bank5[:, :]
        ps_u = bank67[:, 0:512]
        ps_g = bank67[:, 512:1024]
        ps_xt = bank01[:, 0:PS]
        ps_y = bank67[:, 0:PS]
        ps_h = [bank2, bank3, bank4]
        ps_o = bank5[:, 0:CAP]

        ident = sb("ident", [P, P])
        tri = sb("tri", [P, T])
        tri_b = sb("tri_b", [P, P], bf16)
        ones_b = sb("ones_b", [P, P], bf16)
        eps = sb("eps", [P, 4])
        rev_i = sb("rev_i", [P, NJ * NE], i32)
        rev = sb("rev", [P, NJ, NE])
        tokid = sb("tokid", [P, NTOK // P], i32)
        blank = sb("blank", [P, ROW])

        c_sb = sb("c_sb", [NB, D])
        c_e = sb("c_e", [NB, D])
        c_s = sb("c_s", [NB, D])
        c_T = sb("c_T", [P, NB])
        wmod = sb("wmod", [P, 6, D])
        mod = sb("mod", [P, 6, NB])
        mod_r = sb("mod_r", [P, 6, NB])
        sgn = sb("sgn", [P, 2, NB])
        wqkv = sb("wqkv", [P, 3, D])
        wqkvT = sb("wqkvT", [P, 3 * D])
        wsw = sb("wsw", [P, 2, D])
        wswT = sb("wswT", [P, 2 * D])
        wout = sb("wout", [P, D])
        gw = sb("gw", [NE, D])
        gwT = sb("gwT", [P, NE])
        diag_ga = sb("diag_ga", [P, NB, D])
        diag_gb = sb("diag_gb", [P, NB, D])
        woga = sb("woga", [P, NB, D])
        gb_row = sb("gb_row", [P, NB, D])

        x_all = sb("x_all", [P, NB, NJ, D])
        rows = sb("rows", [P, NB, NJ, ROW])
        st1 = sb("st1", [P, NJ, 6])
        mv1 = sb("mv1", [P, NJ, 2])
        ln1 = sb("ln1", [P, NJ])
        rs1 = sb("rs1", [P, NJ])
        xh = sb("xh", [P, NJ, D])
        hT = [sb(f"hT{n}", [P, T]) for n in range(2)]
        hsq = sb("hsq", [P, T])
        ssq = sb("ssq", [P, NJ, 2])
        junk = sb("junk", [P, 2 * NJ, D])
        mh = sb("mh", [P, NJ])
        nrm = sb("nrm", [P, 3 * NJ])
        nrl = sb("nrl", [P, 3 * NJ])
        nrr = sb("nrr", [P, 3 * NJ])
        qkn = sb("qkn", [P, 2 * NJ, D])
        ew = [sb(f"ew{n}", [P, NJ, 2, D]) for n in range(2)]
        kv = [sb(f"kv{n}", [P, NJ, D]) for n in range(2)]
        lq = sb("lq", [P, T])
        lw = sb("lw", [P, T])
        lden = sb("lden", [P, T])
        rden = sb("rden", [P, T])
        yT = sb("yT", [P, T])
        gc = sb("gc", [P, T])
        eg = sb("eg", [P, T])
        lg = sb("lg", [P, T])
        sg = sb("sg", [P, T])
        gs = sb("gs", [P, T])
        GT = [sb(f"GT{n}", [P, T]) for n in range(2)]
        st2 = sb("st2", [P, NJ, 6])
        mv2 = sb("mv2", [P, NJ, 2])
        ln2 = sb("ln2", [P, NJ])
        rs2 = sb("rs2", [P, NJ])
        xh2 = sb("xh2", [P, NJ, D])
        h2T = sb("h2T", [P, T])
        mx = sb("mx", [P, NJ])
        dl = sb("dl", [P, NJ, NE])
        pe_ = sb("pe_", [P, NJ, NE])
        psm = sb("psm", [P, NJ])
        prob = sb("prob", [P, NJ])
        cand = sb("cand", [P, NJ, NE])
        best = sb("best", [P, NJ])
        oh = sb("oh", [P, NJ, NE], bf16)
        ohs = sb("ohs", [P, NE])
        seen = sb("seen", [P, NE], bf16)
        rk = sb("rk", [P, NJ, NE])
        rank = sb("rank", [P, NJ])
        sl_a = sb("sl_a", [P, NJ])
        sl_o = sb("sl_o", [P, NJ])
        slot = sb("slot", [P, NB, NJ], i32)

        w1 = [sb(f"w1_{n}", [P, 2, FF]) for n in range(2)]
        w2 = [sb(f"w2_{n}", [P, 2, NF, D]) for n in range(2)]
        hin = [sb(f"hin{n}", [P, NS, D]) for n in range(2)]
        rest = [sb(f"rest{n}", [P, NS, ROW - D]) for n in range(2)]
        XT = [sb(f"XT{n}", [P, PS]) for n in range(2)]
        HT = [sb(f"HT{n}", [P, NF, CAP]) for n in range(2)]
        OT = qkn[:, 0:NS, :].rearrange("p n d -> p (n d)")
        yw = junk[:, 0:NS, :]
        fin = [sb(f"fin{n}", [P, NS, D]) for n in range(2)]

        x_in = [sem(f"x_in{n}") for n in range(4)]
        c_in, w_in, blank_out = sem("c_in"), sem("w_in"), sem("blank_out")
        consts, c_step, mod_ps, mod_step, mod_done = [
            sem(n) for n in ("consts", "c_step", "mod_ps", "mod_step", "mod_done")]
        pool_setup = sem("pool_setup")
        wt_ps, wt_done, diag_done, row_ps, row_done = [
            sem(n) for n in ("wt_ps", "wt_done", "diag_done", "row_ps", "row_done")]
        (ln1_st, ln1_mv, ln1_ln, ln1_rs, xh_done, xhT_ps, hT_done, hsq_done, mh_ps, mh_done,
         res_ps, res_done, qk_ps, v_ps, ssq_done, nrm_a, nrm_b, nrl_done, nrr_done, qkn_done,
         ew_done, kv_done) = [sem(n) for n in (
             "ln1_st", "ln1_mv", "ln1_ln", "ln1_rs", "xh_done", "xhT_ps", "hT_done", "hsq_done",
             "mh_ps", "mh_done", "res_ps", "res_done", "qk_ps", "v_ps", "ssq_done", "nrm_a",
             "nrm_b", "nrl_done", "nrr_done", "qkn_done", "ew_done", "kv_done")]
        (eqT_ps, sumw_ps, sumkv_ps, lq_done, lw_done, lden_done, rden_done, yT_done, u_ps, g_ps,
         gc_done, eg_done, lg_done, sg_done, gs_done, GT_done) = [sem(n) for n in (
             "eqT_ps", "sumw_ps", "sumkv_ps", "lq_done", "lw_done", "lden_done", "rden_done",
             "yT_done", "u_ps", "g_ps", "gc_done", "eg_done", "lg_done", "sg_done", "gs_done",
             "GT_done")]
        (x1_ps, x1_done, ln2_st, ln2_mv, ln2_ln, ln2_rs, xh2_done, xh2T_ps, h2T_done, h2_ps,
         h2_done, logit_ps, mx_done, dl_done, pe_done, psm_done, prob_done, cand_done, best_done,
         oh_done, ohs_done, seen_done, rank_ps, rk_done, rank_done, sl_done, slot_done,
         gp_done) = [sem(n) for n in (
             "x1_ps", "x1_done", "ln2_st", "ln2_mv", "ln2_ln", "ln2_rs", "xh2_done", "xh2T_ps",
             "h2T_done", "h2_ps", "h2_done", "logit_ps", "mx_done", "dl_done", "pe_done",
             "psm_done", "prob_done", "cand_done", "best_done", "oh_done", "ohs_done",
             "seen_done", "rank_ps", "rk_done", "rank_done", "sl_done", "slot_done", "gp_done")]
        dve_past, pool_past = sem("dve_past"), sem("pool_past")
        x1_out, scattered = sem("x1_out"), sem("scattered")
        wts_in = [sem(f"wts_in{n}") for n in range(2)]
        hin_in = [sem(f"hin_in{n}") for n in range(2)]
        rest_in = [sem(f"rest_in{n}") for n in range(2)]
        final_out = [sem(f"final_out{n}") for n in range(2)]
        xt_ps, xt_done, h_ps, h_done, o_ps, o_done, y_ps, yw_done, fin_done = [
            sem(n) for n in ("xt_ps", "xt_done", "h_ps", "h_done", "o_ps", "o_done", "y_ps",
                             "yw_done", "fin_done")]

        def after(eng, s, b, lag=0):
            if isinstance(b, int) and b - lag < 0:
                return
            eng.wait_ge(s, b + 1 - lag)

        def carry_waits(eng, s):
            eng.sem_inc(s, 1)

        def steps(eng, chains):
            depth = max(lag for lag, _ in chains)
            lo, hi = 4, NB

            def peeled(i):
                for lag, chain in chains:
                    if 0 <= i - lag < NB:
                        chain(i - lag, (i - lag) % 2)

            for i in range(lo):
                peeled(i)
            with eng.Fori(lo // 2, hi // 2) as p:
                for u in range(2):
                    for lag, chain in chains:
                        chain(2 * p + (u - lag), (u - lag) % 2)
            for i in range(hi, NB + depth):
                peeled(i)

        def in_pairs(eng, chain):
            for i in range(2):
                chain(i, i % 2, i // 2)
            with eng.Fori(1, NPAIR // 2 - 1) as p:
                for u in range(2):
                    chain(2 * p + u, u, p)
            for i in range(NPAIR - 2, NPAIR):
                chain(i, i % 2, i // 2)

        block = ctx.enter_context(nc.Block())

        @block.sync
        def _(sp):
            sp.dma_start(c_sb[:, :], c_d).then_inc(c_in, 16)
            x_v = x_d.rearrange("b (j p) d -> p b j d", p=P)
            xs = [(0, 1), (1, 2), (2, 4), (4, NB)]
            sp.dma_start(x_all[:, 0, :, :], x_v[:, 0, :, :]).then_inc(x_in[0], 16)
            sp.dma_start(wmod[:, :, :], wmod_d.rearrange("i (m d) -> i m d", m=6)).then_inc(c_in, 16)
            sp.dma_start(wqkv[:, :, :], w_qkv_d.rearrange("(m e) d -> e m d", m=3)).then_inc(w_in, 16)
            sp.dma_start(wsw[:, :, :], w_swiglu_d.rearrange("(m e) d -> e m d", m=2)).then_inc(w_in, 16)
            sp.dma_start(wout[:, :], w_out_d).then_inc(w_in, 16)
            sp.dma_start(gw[:, :], gate_w_d).then_inc(w_in, 16)
            for n in range(1, 4):
                lo, hi = xs[n]
                for b in range(lo, hi):
                    sp.dma_start(x_all[:, b, :, :], x_v[:, b, :, :]).then_inc(x_in[n], 16)
            sp.wait_ge(pool_setup, 8)
            disp_v = disp_d.rearrange("(n p) c -> p n c", p=P)
            for q in range(NPAIR):
                sp.dma_start(disp_v[:, q * NS:(q + 1) * NS, :],
                             blank[:, :].unsqueeze(1).to_broadcast([P, NS, ROW])).then_inc(blank_out, 16)

            def load_weights(i, par):
                sp.dma_start(w1[par][:, :, :], w1_d[bass.ds(2 * i, 2), :, :].rearrange("e d f -> d e f")
                             ).then_inc(wts_in[par], 16)
                sp.dma_start(w2[par][:, 0, :, :], w2_d[bass.ds(2 * i, 1), :, :].rearrange(
                    "e (f p) d -> p (e f) d", p=P)).then_inc(wts_in[par], 16)
                sp.dma_start(w2[par][:, 1, :, :], w2_d[bass.ds(2 * i + 1, 1), :, :].rearrange(
                    "e (f p) d -> p (e f) d", p=P)).then_inc(wts_in[par], 16)

            for i in range(2):
                load_weights(i, i)
            for b in range(NB):
                sp.wait_ge(x1_done, b + 1)
                sp.dma_start(out_d[b, :, :].rearrange("(j p) d -> p j d", p=P),
                             rows[:, b, :, C_X1:C_X1 + D]).then_inc(x1_out, 16)
            sp.wait_ge(scattered, 16 * NB * NJ)

            def load_slots(i, par, k):
                if not isinstance(i, int) or i >= 2:
                    sp.wait_ge(xt_ps, i - 1)
                src = disp_d[bass.ds(i * PS, PS), :].rearrange("(n p) c -> p n c", p=P)
                sp.dma_start(hin[par][:, :, :], src[:, :, 0:D]).then_inc(hin_in[par], 16)
                if not isinstance(i, int) or i >= 2:
                    sp.wait_ge(final_out[par], 16 * NS * k)
                sp.dma_start(rest[par][:, :, :], src[:, :, D:ROW]).then_inc(rest_in[par], 16)
                if not isinstance(i, int) or i >= 2:
                    sp.wait_ge(o_ps, 2 * i - 2)
                    load_weights(i, par)

            in_pairs(sp, load_slots)
            sp.wait_ge(x1_out, 16 * NB)
            for par in range(2):
                sp.wait_ge(final_out[par], 16 * NS * NPAIR // 2)

        @block.gpsimd
        def _(pool):
            pool.memset(ident[:, :], 0.0).then_inc(pool_setup, 1)
            pool.memset(tri[:, :], 1.0).then_inc(pool_setup, 1)
            pool.memset(blank[:, :], 0.0).then_inc(pool_setup, 1)
            pool.memset(ones_b[:, :], 1.0).then_inc(pool_setup, 1)
            pool.memset(seen[:, :], 0.0).then_inc(pool_setup, 1)
            pool.iota(rev_i[:, :], pattern=[[0, NJ], [-1, NE]], base=NE, channel_multiplier=0
                      ).then_inc(pool_setup, 1)
            pool.iota(tokid[:, :], pattern=[[P, NTOK // P]], base=0, channel_multiplier=1
                      ).then_inc(pool_setup, 1)
            pool.wait_ge(pool_setup, 7)
            pool.memset(blank[:, C_TOK:C_TOK + 1].bitcast(i32), NOWHERE).then_inc(pool_setup, 1)
            pool.affine_select(out=ident[:, :], in_=ident[:, :], compare_op=ALU.not_equal, fill=1.0,
                               base=0, pattern=[[-1, P]], channel_multiplier=1).then_inc(consts, 1)
            pool.affine_select(out=tri[:, 0:P], in_=tri[:, 0:P], compare_op=ALU.is_ge, fill=0.0,
                               base=0, pattern=[[1, P]], channel_multiplier=-1).then_inc(consts, 1)
            pool.wait_ge(consts, 2)
            pool.tensor_copy(tri_b[:, :], tri[:, 0:P]).then_inc(consts, 1)
            rows_t = rows[:, :, :, :].rearrange("p b j c -> p (b j) c")
            pool.tensor_copy(rows_t[:, :, C_TOK].bitcast(i32), tokid[:, :])
            pool.memset(rows_t[:, :, C_TOK + 1], 0.0)
            pool.tensor_copy(rev[:, :, :].rearrange("p j e -> p (j e)"), rev_i[:, :]).then_inc(consts, 1)

            def qkv(b, par):
                after(pool, hT_done, b)
                after(pool, mh_ps, b, 1)
                pool.tensor_tensor(hsq[:, :], hT[par][:, :], hT[par][:, :], ALU.mult
                                   ).then_inc(hsq_done, 1)

            def mix(b, par):
                after(pool, lq_done, b)
                after(pool, lw_done, b)
                after(pool, rden_done, b, 1)
                pool.tensor_tensor(lden[:, :], lq[:, :], lw[:, :], ALU.add).then_inc(lden_done, 1)
                after(pool, gc_done, b)
                after(pool, sg_done, b)
                after(pool, GT_done, b, 1)
                pool.tensor_tensor(gs[:, :], gc[:, :], sg[:, :], ALU.mult).then_inc(gs_done, 1)

            def route(b, par):
                after(pool, prob_done, b)
                for j in range(NJ):
                    last = pool.tensor_scalar(rows[:, b, j, C_GP:C_GP + D], gb_row[:, b, :],
                                              prob[:, j:j + 1], None, ALU.mult)
                last.then_inc(gp_done, 1)
                pool.wait_ge(gp_done, b + 1)
                after(pool, h2_done, b)
                after(pool, slot_done, b)
                for j in range(NJ):
                    pool.indirect_dma_start(
                        out=disp_d, out_offset=bass.IndirectOffsetOnAxis(ap=slot[:, b, j:j + 1], axis=0),
                        in_=rows[:, b, j, :], in_offset=None, bounds_check=NSLOT - 1,
                        oob_is_err=False).then_inc(scattered, 16)

            pool.wait_ge(row_done, 4)
            for i in range(NB + 3):
                if i == 3:
                    pool.wait_ge(blank_out, 16 * NPAIR)
                if 0 <= i - 3 < NB:
                    route(i - 3, (i - 3) % 2)
                if 0 <= i - 2 < NB:
                    mix(i - 2, i % 2)
                if i < NB:
                    qkv(i, i % 2)

            pool.wait_ge(x1_out, 16 * NB)

            last_token = pool.to_reg(NTOK - 1)

            def send(i, par, k):
                after(pool, fin_done, i)
                carry_waits(pool, pool_past)
                for n in range(NS):
                    pool.indirect_dma_start(
                        out=out_d.rearrange("b t d -> (b t) d"),
                        out_offset=bass.IndirectOffsetOnAxis(
                            ap=rest[par][:, n, C_TOK - D:C_TOK - D + 1].bitcast(i32), axis=0),
                        in_=fin[par][:, n, :], in_offset=None, bounds_check=last_token,
                        oob_is_err=False).then_inc(final_out[par], 16)

            in_pairs(pool, send)

        @block.scalar
        def _(act):
            act.preload_act_table_set("natural_log_exp_and_others")
            act.wait_ge(c_in, 32)
            act.activation(c_e[:, :], c_sb[:, :], ACT.Exp, scale=-1.0).then_inc(c_step, 1)
            act.wait_ge(wt_ps, 1)
            act.mul(wqkvT[:, 0:D], bank01[:, 0:D], -1.0)
            act.copy(wqkvT[:, D:3 * D], bank01[:, D:3 * D])
            act.copy(wswT[:, :], bank01[:, 512:512 + 2 * D])
            act.copy(gwT[:, :], bank01[:, 512 + 2 * D:512 + 2 * D + NE]).then_inc(wt_done, 1)
            for n, (dst, src) in enumerate(((woga, bank3), (woga, bank4), (gb_row, bank5), (gb_row, bank67))):
                act.wait_ge(row_ps, n + 1)
                act.copy(dst[:, 4 * (n % 2):4 * (n % 2) + 4, :],
                         src[:, 0:512].rearrange("p (b d) -> p b d", d=D)).then_inc(row_done, 1)

            def ln(b, par):
                after(act, ln1_mv, b)
                act.activation(ln1[:, :], mv1[:, :, 1], ACT.Ln, bias=eps[:, 0:1]).then_inc(ln1_ln, 1)
                act.wait_ge(ln1_ln, b + 1)
                after(act, xh_done, b, 1)
                act.activation(rs1[:, :], ln1[:, :], ACT.Exp, scale=-0.5).then_inc(ln1_rs, 1)
                after(act, xhT_ps, b)
                after(act, res_ps, b, 2)
                after(act, v_ps, b, 2)
                after(act, hsq_done, b, 2)
                act.activation(hT[par][:, :], ps_t, ACT.Identity, bias=mod[:, SA, bass.ds(b, 1)],
                               scale=mod[:, CA, bass.ds(b, 1)]).then_inc(hT_done, 1)

            def qkv(b, par):
                after(act, qk_ps, b)
                after(act, nrm_b, b, 1)
                for j in range(NJ):
                    for m in range(2):
                        last = act.activation(junk[:, 2 * j + m, :], ps_qk[:, j, m * D:(m + 1) * D], ACT.Square,
                                              accum_out=ssq[:, j, m:m + 1])
                last.then_inc(ssq_done, 1)
                after(act, nrm_b, b)
                act.activation(nrl[:, :], nrm[:, :], ACT.Ln).then_inc(nrl_done, 1)
                act.wait_ge(nrl_done, b + 1)
                after(act, kv_done, b, 1)
                act.activation(nrr[:, :], nrl[:, :], ACT.Exp, scale=-0.5).then_inc(nrr_done, 1)
                after(act, qkn_done, b)
                after(act, eqT_ps, b, 2)
                after(act, sumw_ps, b, 2)
                act.activation(ew[par][:, :, :, :].rearrange("p j m d -> p (j m) d"), qkn[:, :, :],
                               ACT.Exp).then_inc(ew_done, 1)

            def mix(b, par):
                after(act, eqT_ps, b)
                after(act, lden_done, b, 1)
                act.activation(lq[:, :], ps_g, ACT.Ln, bias=eps[:, 2:3]).then_inc(lq_done, 1)
                after(act, sumw_ps, b)
                act.activation(lw[:, :], ps_w, ACT.Ln, bias=eps[:, 1:2]).then_inc(lw_done, 1)
                after(act, lden_done, b)
                after(act, yT_done, b, 1)
                act.activation(rden[:, :], lden[:, :], ACT.Exp, scale=-1.0).then_inc(rden_done, 1)
                after(act, gc_done, b)
                act.activation(eg[:, :], gc[:, :], ACT.Exp, scale=-1.0).then_inc(eg_done, 1)
                act.wait_ge(eg_done, b + 1)
                act.activation(lg[:, :], eg[:, :], ACT.Ln, bias=eps[:, 2:3]).then_inc(lg_done, 1)
                act.wait_ge(lg_done, b + 1)
                after(act, gs_done, b, 1)
                act.activation(sg[:, :], lg[:, :], ACT.Exp, scale=-1.0).then_inc(sg_done, 1)

            def route(b, par):
                after(act, ln2_mv, b)
                act.activation(ln2[:, :], mv2[:, :, 1], ACT.Ln, bias=eps[:, 0:1]).then_inc(ln2_ln, 1)
                act.wait_ge(ln2_ln, b + 1)
                act.activation(rs2[:, :], ln2[:, :], ACT.Exp, scale=-0.5).then_inc(ln2_rs, 1)
                after(act, xh2T_ps, b)
                act.activation(h2T[:, :], ps_t, ACT.Identity, bias=mod[:, SB, bass.ds(b, 1)],
                               scale=mod[:, CB, bass.ds(b, 1)]).then_inc(h2T_done, 1)
                after(act, h2_ps, b)
                act.copy(rows[:, b, :, 0:D], ps_t.rearrange("p (j d) -> p j d", d=D)).then_inc(h2_done, 1)
                after(act, dl_done, b)
                act.activation(pe_[:, :, :], dl[:, :, :], ACT.Exp).then_inc(pe_done, 1)

            act.wait_ge(mod_done, 1)
            steps(act, [(3, route), (2, mix), (1, qkv), (0, ln)])

            HB = 3

            def experts(i, par, k):
                for c in range(2 * NF):
                    e, f = c // NF, c % NF
                    act.wait_ge(h_ps, 2 * NF * i + c + 1)
                    if f == 0 and (not isinstance(i, int) or i >= 1):
                        act.wait_ge(o_ps, 2 * i - 1 + e)
                    act.activation(HT[e][:, f, :], ps_h[c % HB][:, 0:CAP], ACT.Gelu_apprx_tanh
                                   ).then_inc(h_done, 1)

            in_pairs(act, experts)

        @block.vector
        def _(dve):
            dve.memset(eps[:, 0:1], EPS_LN)
            dve.memset(eps[:, 1:2], 1e-06)
            dve.memset(eps[:, 2:4], 1.0).then_inc(mod_step, 1)
            dve.wait_ge(c_step, 1)
            dve.tensor_scalar(c_e[:, :], c_e[:, :], 1.0, None, ALU.add).then_inc(c_step, 1)
            dve.wait_ge(c_step, 2)
            dve.reciprocal(c_e[:, :], c_e[:, :]).then_inc(c_step, 1)
            dve.wait_ge(c_step, 3)
            dve.tensor_tensor(c_s[:, :], c_sb[:, :], c_e[:, :], ALU.mult).then_inc(c_step, 1)
            dve.wait_ge(mod_ps, 1)
            dve.tensor_copy(c_T[:, :], bank2[:, 0:NB]).then_inc(c_step, 1)
            dve.wait_ge(mod_ps, 2)
            dve.tensor_copy(mod_r[:, :, :], bank2[:, 64:64 + 6 * NB].rearrange("p (m b) -> p m b", m=6)
                            ).then_inc(mod_step, 1)
            dve.wait_ge(mod_step, 2)
            for n, m in enumerate((GA, GB)):
                dve.tensor_scalar(sgn[:, n, :], mod_r[:, m, :], 0.0, 2.0, ALU.is_ge, ALU.mult)
                dve.tensor_scalar(mod[:, m, :], mod_r[:, m, :], -1.0, None, ALU.mult)
            for m in (CA, CB):
                dve.tensor_scalar(mod[:, m, :], mod_r[:, m, :], 1.0, None, ALU.add)
            dve.tensor_copy(mod[:, SA, :], mod_r[:, SA, :])
            dve.tensor_copy(mod[:, SB, :], mod_r[:, SB, :]).then_inc(mod_step, 1)
            dve.wait_ge(mod_step, 3)
            for m in (GA, GB):
                last = dve.tensor_tensor(mod[:, m, :], mod[:, m, :], mod_r[:, m, :], ALU.max)
            last.then_inc(mod_step, 1)
            dve.wait_ge(mod_step, 4)
            for m in (GA, GB):
                last = dve.tensor_scalar(mod[:, m, :], mod[:, m, :], 0.25, None, ALU.max)
            last.then_inc(mod_step, 1)
            dve.wait_ge(mod_step, 5)
            for n, m in enumerate((GA, GB)):
                last = dve.scalar_tensor_tensor(mod[:, m, :], sgn[:, n, :], -1.0, mod[:, m, :],
                                                ALU.add, ALU.mult)
            last.then_inc(mod_done, 1)
            dve.wait_ge(mod_done, 1)
            dve.wait_ge(consts, 1)
            for dst, m in ((diag_ga, GA), (diag_gb, GB)):
                dve.tensor_tensor(dst[:, :, :], ident[:, :].unsqueeze(1).to_broadcast([P, NB, D]),
                                  mod[:, m, :].unsqueeze(2).to_broadcast([P, NB, D]), ALU.mult
                                  ).then_inc(diag_done, 1)

            def normalize(b, src, dst, mv, rs, done):
                for j in range(NJ):
                    last = dve.tensor_scalar(dst[:, j, :], src[:, j, :], mv[:, j, 0:1], rs[:, j:j + 1],
                                             ALU.subtract, ALU.mult)
                last.then_inc(done, 1)

            def ln(b, par):
                xb = x_all[:, b, :, :]
                for j in range(NJ):
                    last = dve.bn_stats(st1[:, j, :], x_all[:, b, j, :])
                last.then_inc(ln1_st, 1)
                dve.wait_ge(ln1_st, b + 1)
                after(dve, ln1_ln, b, 1)
                carry_waits(dve, dve_past)
                for j in range(NJ):
                    last = dve.bn_aggr(mv1[:, j, :], st1[:, j, :])
                last.then_inc(ln1_mv, 1)
                after(dve, ln1_rs, b)
                after(dve, xhT_ps, b, 1)
                for j in range(NJ):
                    last = dve.tensor_scalar(xh[:, j, :], x_all[:, b, j, :], mv1[:, j, 0:1],
                                             rs1[:, j:j + 1], ALU.subtract, ALU.mult)
                last.then_inc(xh_done, 1)
                after(dve, res_ps, b)
                dve.wait_ge(xh_done, b + 1)
                dve.tensor_tensor(x_all[:, b, :, :], x_all[:, b, :, :],
                                  ps_v, ALU.add).then_inc(res_done, 1)
                after(dve, mh_ps, b)
                after(dve, nrl_done, b, 1)
                dve.tensor_scalar(nrm[:, 2 * NJ:3 * NJ], ps_t[:, 0:NJ], 1.0 / D, EPS_RMS, ALU.mult, ALU.add
                                  ).then_inc(mh_done, 1)
                dve.wait_ge(mh_done, b + 1)
                dve.tensor_scalar(mh[:, :], nrm[:, 2 * NJ:3 * NJ], EPS_RMS, None, ALU.mult
                                  ).then_inc(nrm_a, 1)

            def qkv(b, par):
                after(dve, ssq_done, b)
                dve.wait_ge(nrm_a, b + 1)
                dve.scalar_tensor_tensor(nrm[:, 0:2 * NJ].rearrange("p (j m) -> p j m", m=2), ssq[:, :, :],
                                         1.0 / D, mh[:, :].unsqueeze(2).to_broadcast([P, NJ, 2]),
                                         ALU.mult, ALU.add).then_inc(nrm_b, 1)
                after(dve, nrr_done, b)
                after(dve, ew_done, b, 1)
                dve.tensor_tensor(qkn[:, :, :], ps_qk.rearrange("p j (m d) -> p (j m) d", m=2),
                                  nrr[:, 0:2 * NJ].unsqueeze(2).to_broadcast([P, 2 * NJ, D]), ALU.mult
                                  ).then_inc(qkn_done, 1)
                after(dve, v_ps, b)
                after(dve, ew_done, b)
                after(dve, sumkv_ps, b, 2)
                for j in range(NJ):
                    last = dve.scalar_tensor_tensor(kv[par][:, j, :], ps_v[:, j, :],
                                                    nrr[:, 2 * NJ + j:2 * NJ + j + 1],
                                                    ew[par][:, j, 1, :], ALU.mult, ALU.mult)
                last.then_inc(kv_done, 1)

            def mix(b, par):
                after(dve, rden_done, b)
                after(dve, sumkv_ps, b)
                after(dve, g_ps, b, 1)
                dve.tensor_tensor(yT[:, :], ps_kv, rden[:, :], ALU.mult).then_inc(yT_done, 1)
                after(dve, g_ps, b)
                after(dve, gs_done, b, 1)
                dve.tensor_scalar(gc[:, :], ps_g, -43.0, None, ALU.max).then_inc(gc_done, 1)
                after(dve, gs_done, b)
                after(dve, u_ps, b)
                after(dve, x1_ps, b, 2)
                dve.tensor_tensor(GT[par][:, :], gs[:, :], ps_u, ALU.mult).then_inc(GT_done, 1)

            def route(b, par):
                after(dve, x1_ps, b)
                dve.wait_ge(res_done, b + 1)
                dve.tensor_tensor(rows[:, b, :, C_X1:C_X1 + D], x_all[:, b, :, :],
                                  ps_u.rearrange("p (j d) -> p j d", d=D), ALU.add).then_inc(x1_done, 1)
                dve.wait_ge(x1_done, b + 1)
                carry_waits(dve, dve_past)
                for j in range(NJ):
                    last = dve.bn_stats(st2[:, j, :], rows[:, b, j, C_X1:C_X1 + D])
                last.then_inc(ln2_st, 1)
                dve.wait_ge(ln2_st, b + 1)
                carry_waits(dve, dve_past)
                for j in range(NJ):
                    last = dve.bn_aggr(mv2[:, j, :], st2[:, j, :])
                last.then_inc(ln2_mv, 1)
                after(dve, ln2_rs, b)
                for j in range(NJ):
                    last = dve.tensor_scalar(xh2[:, j, :], rows[:, b, j, C_X1:C_X1 + D], mv2[:, j, 0:1],
                                             rs2[:, j:j + 1], ALU.subtract, ALU.mult)
                last.then_inc(xh2_done, 1)
                after(dve, logit_ps, b)
                lg_v = ps_g[:, 0:NJ * NE].rearrange("p (j e) -> p j e", e=NE)
                dve.tensor_reduce(mx[:, :], lg_v, X, ALU.max).then_inc(mx_done, 1)
                dve.wait_ge(mx_done, b + 1)
                dve.tensor_tensor(dl[:, :, :], lg_v, mx[:, :].unsqueeze(2).to_broadcast([P, NJ, NE]),
                                  ALU.subtract).then_inc(dl_done, 1)
                dve.wait_ge(dl_done, b + 1)
                dve.scalar_tensor_tensor(cand[:, :, :], dl[:, :, :], 0.0, rev[:, :, :], ALU.is_ge, ALU.mult
                                         ).then_inc(cand_done, 1)
                dve.wait_ge(cand_done, b + 1)
                dve.tensor_reduce(best[:, :], cand[:, :, :], X, ALU.max).then_inc(best_done, 1)
                dve.wait_ge(best_done, b + 1)
                dve.tensor_tensor(oh[:, :, :], rev[:, :, :], best[:, :].unsqueeze(2).to_broadcast([P, NJ, NE]),
                                  ALU.is_equal).then_inc(oh_done, 1)
                after(dve, pe_done, b)
                dve.tensor_reduce(psm[:, :], pe_[:, :, :], X, ALU.add).then_inc(psm_done, 1)
                dve.wait_ge(psm_done, b + 1)
                after(dve, gp_done, b, 1)
                dve.reciprocal(prob[:, :], psm[:, :]).then_inc(prob_done, 1)
                dve.tensor_reduce(ohs[:, :], oh[:, :, :].rearrange("p j e -> p e j"), X, ALU.add
                                  ).then_inc(ohs_done, 1)
                after(dve, rank_ps, b)
                dve.tensor_tensor(rk[:, :, :], oh[:, :, :],
                                  ps_g[:, 64:64 + NJ * NE].rearrange("p (j e) -> p j e", e=NE), ALU.mult
                                  ).then_inc(rk_done, 1)
                dve.wait_ge(ohs_done, b + 1)
                dve.tensor_tensor(seen[:, :], seen[:, :], ohs[:, :], ALU.add).then_inc(seen_done, 1)
                dve.wait_ge(rk_done, b + 1)
                dve.tensor_reduce(rank[:, :], rk[:, :, :], X, ALU.add).then_inc(rank_done, 1)
                dve.wait_ge(rank_done, b + 1)
                dve.scalar_tensor_tensor(sl_a[:, :], best[:, :], -float(CAP), rank[:, :], ALU.mult, ALU.add)
                dve.tensor_scalar(sl_o[:, :], rank[:, :], float(CAP), float(NOWHERE), ALU.is_gt, ALU.mult
                                  ).then_inc(sl_done, 1)
                dve.wait_ge(sl_done, b + 1)
                dve.scalar_tensor_tensor(slot[:, b, :], sl_a[:, :], float(NE * CAP - 1), sl_o[:, :],
                                         ALU.add, ALU.add).then_inc(slot_done, 1)

            dve.wait_ge(wt_done, 1)
            dve.wait_ge(row_done, 4)
            dve.wait_ge(consts, 4)
            for n in range(4):
                dve.wait_ge(x_in[n], 16 * (1, 1, 2, NB - 4)[n])
            steps(dve, [(3, route), (2, mix), (1, qkv), (0, ln)])

            def xt_copy(i, par):
                after(dve, xt_ps, i)
                if not isinstance(i, int) or i >= 2:
                    dve.wait_ge(h_ps, 2 * NF * (i - 1))
                dve.tensor_copy(XT[par][:, :], ps_xt).then_inc(xt_done, 1)

            def combine(i, par, k):
                after(dve, y_ps, i)
                dve.wait_ge(rest_in[par], 16 * (k + 1))
                after(dve, fin_done, i, 1)
                dve.tensor_tensor(yw[:, :, :], ps_y.rearrange("p (n d) -> p n d", d=D),
                                  rest[par][:, :, C_GP - D:C_GP], ALU.mult).then_inc(yw_done, 1)
                dve.wait_ge(yw_done, i + 1)
                if not isinstance(i, int) or i >= 2:
                    dve.wait_ge(final_out[par], 16 * NS * k)
                dve.tensor_tensor(fin[par][:, :, :], yw[:, :, :], rest[par][:, :, C_X1 - D:C_X1],
                                  ALU.add).then_inc(fin_done, 1)

            def experts(i, par, k):
                if not isinstance(i, int) or i >= 1:
                    combine(i - 1, 1 - par, k - 1 + par)
                for e in range(2):
                    dve.wait_ge(o_ps, 2 * i + e + 1)
                    if e == 0:
                        after(dve, y_ps, i, 1)
                    dve.tensor_copy(OT[:, e * CAP:(e + 1) * CAP], ps_o).then_inc(o_done, 1)
                    if e == 0 and not (isinstance(i, int) and i == NPAIR - 1):
                        xt_copy(i + 1, 1 - par)

            xt_copy(0, 0)
            in_pairs(dve, experts)
            combine(NPAIR - 1, 1, NPAIR // 2 - 1)

        @block.tensor
        def _(pe):
            pe.wait_ge(consts, 4)
            pe.wait_ge(w_in, 64)
            for m in range(3):
                pe.transpose(bank01[:, m * D:(m + 1) * D], wqkv[:, m, :], ident[:, :])
            for m in range(2):
                pe.transpose(bank01[:, 512 + m * D:512 + (m + 1) * D], wsw[:, m, :], ident[:, :])
            pe.transpose(bank01[:, 512 + 2 * D:512 + 2 * D + NE], gw[:, :], ident[0:NE, 0:NE]
                         ).then_inc(wt_ps, 1)
            pe.wait_ge(c_step, 4)
            pe.transpose(bank2[:, 0:NB], c_s[:, :], ident[0:NB, 0:NB]).then_inc(mod_ps, 1)
            pe.wait_ge(c_step, 5)
            for m in range(6):
                last = pe.matmul(bank2[:, 64 + m * NB:64 + (m + 1) * NB], wmod[:, m, :], c_T[:, :],
                                 start=True, stop=True)
            last.then_inc(mod_ps, 1)
            pe.wait_ge(diag_done, 2)
            for n, dst in enumerate((bank3, bank4)):
                pe.matmul(dst[:, 0:512], wout[:, :],
                          diag_ga[:, 4 * n:4 * n + 4, :].rearrange("p b d -> p (b d)"),
                          start=True, stop=True).then_inc(row_ps, 1)
            for n, dst in enumerate((bank5, bank67)):
                pe.matmul(dst[:, 0:512], tri[:, P:2 * P],
                          diag_gb[:, 4 * n:4 * n + 4, :].rearrange("p b d -> p (b d)"),
                          start=True, stop=True).then_inc(row_ps, 1)

            def ln(b, par):
                after(pe, xh_done, b)
                after(pe, h2_done, b, 3)
                if not isinstance(b, int) or b >= 1:
                    pe.wait_ge(mh_done, b)
                for j in range(NJ):
                    last = pe.transpose(ps_t[:, j * P:(j + 1) * P], xh[:, j, :], ident[:, :])
                last.then_inc(xhT_ps, 1)
                after(pe, hT_done, b)
                after(pe, kv_done, b, 1)
                for j in range(NJ):
                    last = pe.matmul(ps_v[:, j, :], hT[par][:, j * P:(j + 1) * P], diag_ga[:, b, :],
                                     start=True, stop=True)
                last.then_inc(res_ps, 1)
                after(pe, hsq_done, b)
                for j in range(NJ):
                    last = pe.matmul(ps_t[:, j:j + 1], hsq[:, j * P:(j + 1) * P], tri[:, P:P + 1],
                                     start=True, stop=True)
                last.then_inc(mh_ps, 1)

            def qkv(b, par):
                after(pe, qkn_done, b, 1)
                for j in range(NJ):
                    last = pe.matmul(ps_qk[:, j, :], hT[par][:, j * P:(j + 1) * P], wqkvT[:, 0:2 * D],
                                     start=True, stop=True)
                last.then_inc(qk_ps, 1)
                after(pe, res_done, b)
                for j in range(NJ):
                    last = pe.matmul(ps_v[:, j, :], hT[par][:, j * P:(j + 1) * P], wqkvT[:, 2 * D:3 * D],
                                     start=True, stop=True)
                last.then_inc(v_ps, 1)

            def mix(b, par):
                after(pe, ew_done, b)
                after(pe, rk_done, b, 1)
                for j in range(NJ):
                    last = pe.transpose(ps_g[:, j * P:(j + 1) * P], ew[par][:, j, 0, :], ident[:, :])
                last.then_inc(eqT_ps, 1)
                after(pe, lw_done, b, 1)
                for j in range(NJ):
                    last = pe.matmul(ps_w[:, j * P:T], ew[par][:, j, 1, :], tri[:, 0:T - j * P],
                                     start=(j == 0), stop=(j == NJ - 1))
                last.then_inc(sumw_ps, 1)
                after(pe, kv_done, b)
                after(pe, yT_done, b, 1)
                for j in range(NJ):
                    last = pe.matmul(ps_kv[:, j * P:T], kv[par][:, j, :], tri[:, 0:T - j * P],
                                     start=(j == 0), stop=(j == NJ - 1))
                last.then_inc(sumkv_ps, 1)
                after(pe, yT_done, b)
                after(pe, lq_done, b)
                after(pe, x1_done, b, 1)
                pe.matmul(ps_g, wswT[:, D:2 * D], yT[:, :], start=True, stop=True).then_inc(g_ps, 1)
                pe.matmul(ps_u, wswT[:, 0:D], yT[:, :], start=True, stop=True).then_inc(u_ps, 1)

            def x1(b, par):
                after(pe, GT_done, b)
                for j in range(NJ):
                    last = pe.matmul(ps_u[:, j * P:(j + 1) * P], GT[par][:, j * P:(j + 1) * P],
                                     woga[:, b, :], start=True, stop=True)
                last.then_inc(x1_ps, 1)

            def route(b, par):
                x1(b, par)
                after(pe, xh2_done, b)
                pe.wait_ge(mh_done, min(b + 3, NB) if isinstance(b, int) else b + 3)
                for j in range(NJ):
                    last = pe.transpose(ps_t[:, j * P:(j + 1) * P], xh2[:, j, :], ident[:, :])
                last.then_inc(xh2T_ps, 1)
                after(pe, h2T_done, b)
                for j in range(NJ):
                    last = pe.matmul(ps_g[:, j * NE:(j + 1) * NE], h2T[:, j * P:(j + 1) * P], gwT[:, :],
                                     start=True, stop=True)
                last.then_inc(logit_ps, 1)
                for j in range(NJ):
                    last = pe.transpose(ps_t[:, j * P:(j + 1) * P], h2T[:, j * P:(j + 1) * P], ident[:, :])
                last.then_inc(h2_ps, 1)
                after(pe, oh_done, b)
                if not isinstance(b, int) or b >= 1:
                    pe.wait_ge(seen_done, b)
                pe.matmul(ps_g[:, 64:64 + NJ * NE], ones_b[:, :],
                          seen[:, :].unsqueeze(1).to_broadcast([P, NJ, NE]), start=True, stop=False)
                pe.matmul(ps_g[:, 64:64 + NJ * NE], tri_b[:, :], oh[:, :, :].rearrange("p j e -> p (j e)"),
                          start=False, stop=False)
                for j in range(NJ - 1):
                    last = pe.matmul(ps_g[:, 64 + (j + 1) * NE:64 + NJ * NE], ones_b[:, :],
                                     oh[:, j, :].unsqueeze(1).to_broadcast([P, NJ - 1 - j, NE]),
                                     start=False, stop=(j == NJ - 2))
                last.then_inc(rank_ps, 1)

            pe.wait_ge(row_done, 4)
            pe.wait_ge(wt_done, 1)
            steps(pe, [(3, route), (2, mix), (1, qkv), (0, ln)])

            HB = 3

            def xt(i, par, k):
                pe.wait_ge(hin_in[par], 16 * (k + 1))
                after(pe, xt_done, i, 1)
                for n in range(NS):
                    last = pe.transpose(ps_xt[:, n * P:(n + 1) * P], hin[par][:, n, :], ident[:, :])
                last.then_inc(xt_ps, 1)

            def rows_back(i):
                pe.wait_ge(o_done, 2 * i + 2)
                after(pe, yw_done, i, 1)
                for n in range(NS):
                    last = pe.transpose(ps_y[:, n * P:(n + 1) * P], OT[:, n * P:(n + 1) * P], ident[:, :])
                last.then_inc(y_ps, 1)

            def experts(i, par, k):
                first = isinstance(i, int) and i == 0
                after(pe, xt_done, i)
                pe.wait_ge(wts_in[par], 48 * (k + 1))
                for c in range(2 * NF):
                    e, f = c // NF, c % NF
                    if c >= HB:
                        pe.wait_ge(h_done, 2 * NF * i + c - HB + 1)
                    elif not first:
                        back = max(q for q in range(2 * NF) if q % HB == c)
                        pe.wait_ge(h_done, 2 * NF * i + (back - 2 * NF + 1))
                    pe.matmul(ps_h[c % HB][:, 0:CAP], w1[par][:, e, f * P:(f + 1) * P],
                              XT[par][:, e * CAP:(e + 1) * CAP], start=True, stop=True).then_inc(h_ps, 1)
                    if c == NF - 1 and not first:
                        rows_back(i - 1)
                for e in range(2):
                    pe.wait_ge(h_done, 2 * NF * i + (e + 1) * NF)
                    if e == 1 or not first:
                        pe.wait_ge(o_done, 2 * i + e)
                    for f in range(NF):
                        last = pe.matmul(ps_o, w2[par][:, e, f, :], HT[e][:, f, :],
                                         start=(f == 0), stop=(f == NF - 1))
                    last.then_inc(o_ps, 1)
                    if e == 0 and not (isinstance(i, int) and i == NPAIR - 1):
                        xt(i + 1, 1 - par, k + par)

            xt(0, 0, 0)
            in_pairs(pe, experts)
            rows_back(NPAIR - 1)


_INS = ['L0_attn_x', 'L0_attn_w_qkv', 'L0_attn_w_swiglu', 'L0_attn_w_out', 'L0_ffn_gate_w', 'L0_ffn_w1',
        'L0_ffn_w2', 'L0_c', 'L0_wmod']
_OUTS = [((8, 512, 128), 'float32')]


def kernel(**inputs):
    import numpy as _np
    import concourse.bacc as _bacc
    from concourse import mybir as _mybir
    from concourse.bass_utils import run_bass_kernel_spmd as _run

    nc = _bacc.Bacc("TRN2", target_bir_lowering=False, num_devices=1)
    arrays, args = {}, []
    for name in _INS:
        a = _np.ascontiguousarray(inputs[name])
        arrays[f"in_{name}_dram"] = a
        args.append(nc.dram_tensor(f"in_{name}_dram", a.shape, _mybir.dt.from_np(a.dtype), kind="ExternalInput").ap())
    for i, (shape, dtype) in enumerate(_OUTS):
        dt = _mybir.dt.from_np(_np.dtype(dtype))
        args.append(nc.dram_tensor(f"out_{i}_dram", shape, dt, kind="ExternalOutput").ap())
    adaln_attention_moe(nc, *args)
    r = _run(nc, [arrays], core_ids=[0])
    got = tuple(r.results[0][f"out_{i}_dram"] for i in range(len(_OUTS)))
    return got[0]
```

```python
import concourse.bass as bass
from concourse import mybir
from contextlib import ExitStack


def adaln_attention_moe(
    nc: bass.Bass,
    x_d: bass.AP,
    w_qkv_d: bass.AP,
    w_swiglu_d: bass.AP,
    w_out_d: bass.AP,
    gate_w_d: bass.AP,
    w1_d: bass.AP,
    w2_d: bass.AP,
    c_d: bass.AP,
    wmod_d: bass.AP,
    out_d: bass.AP,
):
    f32 = mybir.dt.float32
    bf16 = mybir.dt.bfloat16
    i32 = mybir.dt.int32
    ALU = mybir.AluOpType
    ACT = mybir.ActivationFunctionType
    X = mybir.AxisListType.X

    P = 128
    NB, T, D = x_d.shape
    NJ = T // P
    NTOK = NB * T
    NE, _, FF = w1_d.shape
    NF = FF // P
    CAP = int(1.25 * NTOK / NE)
    CAP += CAP % 2
    NSLOT = NE * CAP
    NPAIR = NE // 2
    PS = 2 * CAP
    NS = PS // P
    EPS_RMS = 1.1920929e-07
    EPS_LN = 1e-05
    NOWHERE = 1 << 20
    C_X1, C_GP, C_TOK, ROW = D, 2 * D, 3 * D, 3 * D + 2
    SA, CA, GA, SB, CB, GB = range(6)

    disp_d = nc.dram_tensor("dispatched_rows", [NSLOT, ROW], f32, kind="Internal").ap()

    ctx = ExitStack()
    with ctx:
        def sb(name, shape, dt=f32):
            return ctx.enter_context(nc.sbuf_tensor(name, shape, dt))

        def sem(name):
            return ctx.enter_context(nc.semaphore(name))

        bank01 = ctx.enter_context(nc.psum_tensor("bank01", [P, 1024], f32))
        bank67 = ctx.enter_context(nc.psum_tensor("bank67", [P, 1024], f32))
        bank2, bank3, bank4, bank5 = [
            ctx.enter_context(nc.psum_tensor(f"bank{n}", [P, 512], f32)) for n in (2, 3, 4, 5)]
        ps_qk = bank01[:, :].rearrange("p (j c) -> p j c", j=NJ)
        ps_t = bank2[:, :]
        ps_rank = bank2[:, 0:NJ * NE]
        ps_v = bank3[:, :].rearrange("p (j c) -> p j c", j=NJ)
        ps_mh = bank3[:, 0:NJ]
        ps_w = bank4[:, :]
        ps_logit = bank4[:, 0:NJ * NE]
        ps_kv = bank5[:, :]
        ps_u = bank67[:, 0:512]
        ps_g = bank67[:, 512:1024]
        ps_xt = bank01[:, 0:PS]
        ps_y = bank67[:, 0:PS]
        ps_h = [bank2, bank3, bank4]
        ps_o = bank5[:, 0:CAP]

        ident = sb("ident", [P, P])
        tri = sb("tri", [P, T])
        tri_b = sb("tri_b", [P, P], bf16)
        ones_b = sb("ones_b", [P, P], bf16)
        eps = sb("eps", [P, 4])
        rev_i = sb("rev_i", [P, NJ * NE], i32)
        rev = sb("rev", [P, NJ, NE])
        tokid = sb("tokid", [P, NTOK // P], i32)
        blank = sb("blank", [P, ROW])

        c_sb = sb("c_sb", [NB, D])
        c_e = sb("c_e", [NB, D])
        c_s = sb("c_s", [NB, D])
        c_T = sb("c_T", [P, NB])
        wmod = sb("wmod", [P, 6, D])
        mod = sb("mod", [P, 6, NB])
        mod_r = sb("mod_r", [P, 6, NB])
        sgn = sb("sgn", [P, 2, NB])
        wqkv = sb("wqkv", [P, 3, D])
        wqkvT = sb("wqkvT", [P, 3 * D])
        wsw = sb("wsw", [P, 2, D])
        wswT = sb("wswT", [P, 2 * D])
        wout = sb("wout", [P, D])
        gw = sb("gw", [NE, D])
        gwT = sb("gwT", [P, NE])
        diag_ga = sb("diag_ga", [P, NB, D])
        diag_gb = sb("diag_gb", [P, NB, D])
        woga = sb("woga", [P, NB, D])
        gb_row = sb("gb_row", [P, NB, D])

        x_all = sb("x_all", [P, NB, NJ, D])
        rows = sb("rows", [P, NB, NJ, ROW])
        st1 = sb("st1", [P, NJ, 6])
        mv1 = sb("mv1", [P, NJ, 2])
        ln1 = sb("ln1", [P, NJ])
        rs1 = sb("rs1", [P, NJ])
        xh = sb("xh", [P, NJ, D])
        NHT = 5
        hT = [sb(f"hT{n}", [P, T]) for n in range(NHT)]
        hsq = sb("hsq", [P, T])
        ssq = sb("ssq", [P, NJ, 2])
        junk = sb("junk", [P, 2 * NJ, D])
        mh = sb("mh", [P, NJ])
        nrm = sb("nrm", [P, 3 * NJ])
        nrl = sb("nrl", [P, 3 * NJ])
        nrr = sb("nrr", [P, 3 * NJ])
        qkn = sb("qkn", [P, 2 * NJ, D])
        ewkv = [sb(f"ewkv{n}", [P, NJ + 1, 3, D]) for n in range(2)]
        lq = sb("lq", [P, T])
        lw = sb("lw", [P, T])
        lden = sb("lden", [P, T])
        rden = sb("rden", [P, T])
        yT = sb("yT", [P, T])
        gc = sb("gc", [P, T])
        eg = sb("eg", [P, T])
        lg = sb("lg", [P, T])
        sg = sb("sg", [P, T])
        gs = sb("gs", [P, T])
        GT = [sb(f"GT{n}", [P, T]) for n in range(2)]
        st2 = sb("st2", [P, NJ, 6])
        mv2 = sb("mv2", [P, NJ, 2])
        ln2 = sb("ln2", [P, NJ])
        rs2 = sb("rs2", [P, NJ])
        nm2 = sb("nm2", [P, NJ])
        xh2 = sb("xh2", [P, NJ, D])
        h2T = sb("h2T", [P, T])
        mx = sb("mx", [P, NJ])
        dl = sb("dl", [P, NJ, NE])
        pe_ = sb("pe_", [P, NJ, NE])
        psm = sb("psm", [P, NJ])
        prob = sb("prob", [P, NJ])
        cand = sb("cand", [P, NJ, NE])
        best = sb("best", [P, NB, NJ])
        oh = [sb(f"oh{n}", [P, NJ, NE], bf16) for n in range(2)]
        ohs = sb("ohs", [P, NE])
        seen = sb("seen", [P, NE], bf16)
        rk = sb("rk", [P, NJ, NE])
        rank = sb("rank", [P, NJ])
        sl_a = sb("sl_a", [P, NJ])
        sl_o = sb("sl_o", [P, NJ])
        slot = sb("slot", [P, NB, NJ], i32)

        w1 = [sb(f"w1_{n}", [P, 2, FF]) for n in range(2)]
        w2 = [sb(f"w2_{n}", [P, 2, NF, D]) for n in range(2)]
        hin = [sb(f"hin{n}", [P, NS, D]) for n in range(2)]
        rest = [sb(f"rest{n}", [P, NS, ROW - D]) for n in range(2)]
        HT = [sb(f"HT{n}", [P, NF, CAP]) for n in range(2)]
        OT = qkn[:, 0:NS, :].rearrange("p n d -> p (n d)")
        yw = junk[:, 0:NS, :]
        x_tiles = x_all[:, :, :, :].rearrange("p b j d -> p (b j) d")
        fin = [x_tiles[:, n * NS:(n + 1) * NS, :] for n in range(2)]
        XT = [x_tiles[:, n * NS:(n + 1) * NS, :].rearrange("p n d -> p (n d)") for n in (2, 3)]

        x_in = [sem(f"x_in{n}") for n in range(NB)]
        c_in, w_in, blank_out = sem("c_in"), sem("w_in"), sem("blank_out")
        consts, c_step, mod_ps, mod_step, mod_done = [
            sem(n) for n in ("consts", "c_step", "mod_ps", "mod_step", "mod_done")]
        pool_setup = sem("pool_setup")
        wt_ps, wt_done, diag_done, row_ps, row_done = [
            sem(n) for n in ("wt_ps", "wt_done", "diag_done", "row_ps", "row_done")]
        (ln1_st, ln1_mv, ln1_ln, ln1_rs, xh_done, xhT_ps, hT_done, hsq_done, mh_ps, mh_done,
         qk_ps, v_ps, ssq_done, nrm_a, nrm_b, nrl_done, nrr_done, qkn_done,
         ew_done, kv_done, pair_done) = [sem(n) for n in (
             "ln1_st", "ln1_mv", "ln1_ln", "ln1_rs", "xh_done", "xhT_ps", "hT_done", "hsq_done",
             "mh_ps", "mh_done", "qk_ps", "v_ps", "ssq_done", "nrm_a",
             "nrm_b", "nrl_done", "nrr_done", "qkn_done", "ew_done", "kv_done", "pair_done")]
        (eqT_ps, sumw_ps, sumkv_ps, lq_done, lw_done, lden_done, rden_done, yT_done, u_ps, g_ps,
         gc_done, eg_done, lg_done, sg_done, gs_done, GT_done) = [sem(n) for n in (
             "eqT_ps", "sumw_ps", "sumkv_ps", "lq_done", "lw_done", "lden_done", "rden_done",
             "yT_done", "u_ps", "g_ps", "gc_done", "eg_done", "lg_done", "sg_done", "gs_done",
             "GT_done")]
        (x1_ps, x1_done, ln2_st, ln2_mv, ln2_ln, ln2_rs, nm2_done, xh2_done, xh2T_ps, h2T_done, h2_ps,
         h2_done, logit_ps, mx_done, dl_done, pe_done, psm_done, prob_done, cand_done, best_done,
         oh_done, ohs_done, seen_done, rank_ps, rk_done, rank_done, sl_done, slot_done,
         gp_done) = [sem(n) for n in (
             "x1_ps", "x1_done", "ln2_st", "ln2_mv", "ln2_ln", "ln2_rs", "nm2_done", "xh2_done", "xh2T_ps",
             "h2T_done", "h2_ps", "h2_done", "logit_ps", "mx_done", "dl_done", "pe_done",
             "psm_done", "prob_done", "cand_done", "best_done", "oh_done", "ohs_done",
             "seen_done", "rank_ps", "rk_done", "rank_done", "sl_done", "slot_done", "gp_done")]
        pool_past = sem("pool_past")
        x1_out, scattered = sem("x1_out"), sem("scattered")
        wts_in = [sem(f"wts_in{n}") for n in range(2)]
        hin_in = [sem(f"hin_in{n}") for n in range(2)]
        rest_in = [sem(f"rest_in{n}") for n in range(2)]
        final_out = [sem(f"final_out{n}") for n in range(2)]
        xt_ps, xt_done, h_ps, h_done, o_ps, o_done, y_ps, yw_done, fin_done = [
            sem(n) for n in ("xt_ps", "xt_done", "h_ps", "h_done", "o_ps", "o_done", "y_ps",
                             "yw_done", "fin_done")]

        def after(eng, s, b, lag=0):
            if isinstance(b, int) and b - lag < 0:
                return
            eng.wait_ge(s, b + 1 - lag)

        def carry_waits(eng, s):
            eng.sem_inc(s, 1)

        def batches(steps, early=(), then=None):
            for i in range(NB + max(lag for lag, _ in steps)):
                for lag, step in steps:
                    if 0 <= i - lag < NB and not (i == lag and step in early):
                        step(i - lag)
                if i == 0 and then:
                    then()

        freed = {bank: (row_done, n + 1) for n, bank in enumerate(("g", "w", "kv", "u"))}

        def claim(pe, bank, reader, b):
            if bank in freed:
                pe.wait_ge(*freed[bank])
            freed[bank] = (reader, b + 1)

        def in_pairs(eng, chain):
            for i in range(2):
                chain(i, i % 2, i // 2)
            with eng.Fori(1, NPAIR // 2 - 1) as p:
                for u in range(2):
                    chain(2 * p + u, u, p)
            for i in range(NPAIR - 2, NPAIR):
                chain(i, i % 2, i // 2)

        block = ctx.enter_context(nc.Block())

        @block.sync
        def _(sp):
            sp.dma_start(c_sb[:, :], c_d).then_inc(c_in, 16)
            x_v = x_d.rearrange("b (j p) d -> p b j d", p=P)
            sp.dma_start(x_all[:, 0, :, :], x_v[:, 0, :, :]).then_inc(x_in[0], 16)
            sp.dma_start(wmod[:, :, :], wmod_d.rearrange("i (m d) -> i m d", m=6)).then_inc(c_in, 16)
            sp.dma_start(wqkv[:, :, :], w_qkv_d.rearrange("(m e) d -> e m d", m=3)).then_inc(w_in, 16)
            sp.dma_start(wsw[:, :, :], w_swiglu_d.rearrange("(m e) d -> e m d", m=2)).then_inc(w_in, 16)
            sp.dma_start(wout[:, :], w_out_d).then_inc(w_in, 16)
            sp.dma_start(gw[:, :], gate_w_d).then_inc(w_in, 16)
            for b in range(1, NB):
                sp.dma_start(x_all[:, b, :, :], x_v[:, b, :, :]).then_inc(x_in[b], 16)
            sp.wait_ge(pool_setup, 8)
            disp_v = disp_d.rearrange("(n p) c -> p n c", p=P)
            for q in range(NPAIR):
                sp.dma_start(disp_v[:, q * NS:(q + 1) * NS, :],
                             blank[:, :].unsqueeze(1).to_broadcast([P, NS, ROW])).then_inc(blank_out, 16)

            def load_weights(i, par):
                sp.dma_start(w1[par][:, :, :], w1_d[bass.ds(2 * i, 2), :, :].rearrange("e d f -> d e f")
                             ).then_inc(wts_in[par], 16)
                sp.dma_start(w2[par][:, :, :, :].rearrange("p e f d -> p e (f d)"),
                             w2_d[bass.ds(2 * i, 2), :, :].rearrange("e (p f) d -> p e (f d)", f=NF)
                             ).then_inc(wts_in[par], 16)

            for i in range(2):
                load_weights(i, i)
            for b in range(NB):
                sp.wait_ge(x1_done, b + 1)
                sp.dma_start(out_d[b, :, :].rearrange("(j p) d -> p j d", p=P),
                             rows[:, b, :, C_X1:C_X1 + D]).then_inc(x1_out, 16)
            sp.wait_ge(scattered, 16 * NB * NJ)

            def load_slots(i, par, k):
                if not isinstance(i, int) or i >= 2:
                    sp.wait_ge(xt_ps, i - 1)
                src = disp_d[bass.ds(i * PS, PS), :].rearrange("(n p) c -> p n c", p=P)
                sp.dma_start(hin[par][:, :, :], src[:, :, 0:D]).then_inc(hin_in[par], 16)
                if not isinstance(i, int) or i >= 2:
                    sp.wait_ge(o_ps, 2 * i - 2)
                    load_weights(i, par)
                    sp.wait_ge(final_out[par], 16 * NS * k)
                sp.dma_start(rest[par][:, :, :], src[:, :, D:ROW]).then_inc(rest_in[par], 16)

            in_pairs(sp, load_slots)
            sp.wait_ge(x1_out, 16 * NB)
            for par in range(2):
                sp.wait_ge(final_out[par], 16 * NS * NPAIR // 2)

        @block.gpsimd
        def _(pool):
            pool.memset(ident[:, :], 0.0).then_inc(pool_setup, 1)
            pool.memset(tri[:, :], 1.0).then_inc(pool_setup, 1)
            pool.memset(blank[:, :], 0.0).then_inc(pool_setup, 1)
            pool.memset(ones_b[:, :], 1.0).then_inc(pool_setup, 1)
            pool.memset(seen[:, :], 0.0).then_inc(pool_setup, 1)
            pool.iota(rev_i[:, :], pattern=[[0, NJ], [-1, NE]], base=NE, channel_multiplier=0
                      ).then_inc(pool_setup, 1)
            pool.iota(tokid[:, :], pattern=[[P, NTOK // P]], base=0, channel_multiplier=1
                      ).then_inc(pool_setup, 1)
            pool.wait_ge(pool_setup, 7)
            pool.memset(blank[:, C_TOK:C_TOK + 1].bitcast(i32), NOWHERE).then_inc(pool_setup, 1)
            pool.affine_select(out=ident[:, :], in_=ident[:, :], compare_op=ALU.not_equal, fill=1.0,
                               base=0, pattern=[[-1, P]], channel_multiplier=1).then_inc(consts, 1)
            pool.affine_select(out=tri[:, 0:P], in_=tri[:, 0:P], compare_op=ALU.is_ge, fill=0.0,
                               base=0, pattern=[[1, P]], channel_multiplier=-1).then_inc(consts, 1)
            pool.wait_ge(consts, 2)
            pool.tensor_copy(tri_b[:, :], tri[:, 0:P]).then_inc(consts, 1)
            rows_t = rows[:, :, :, :].rearrange("p b j c -> p (b j) c")
            pool.tensor_copy(rows_t[:, :, C_TOK].bitcast(i32), tokid[:, :])
            pool.memset(rows_t[:, :, C_TOK + 1], 0.0)
            pool.tensor_copy(rev[:, :, :].rearrange("p j e -> p (j e)"), rev_i[:, :]).then_inc(consts, 1)

            def squares(b):
                after(pool, hT_done, b)
                after(pool, mh_ps, b, 1)
                pool.tensor_tensor(hsq[:, :], hT[b % NHT][:, :], hT[b % NHT][:, :], ALU.mult
                                   ).then_inc(hsq_done, 1)

            def pair_sums(b):
                after(pool, kv_done, b)
                t = ewkv[b % 2]
                pool.tensor_tensor(t[:, NJ, 1:3, :], t[:, 0, 1:3, :], t[:, 1, 1:3, :], ALU.add
                                   ).then_inc(pair_done, 1)

            def log_denominator(b):
                after(pool, lq_done, b)
                after(pool, lw_done, b)
                after(pool, rden_done, b, 1)
                pool.tensor_tensor(lden[:, :], lq[:, :], lw[:, :], ALU.add).then_inc(lden_done, 1)

            def silu(b):
                after(pool, gc_done, b)
                after(pool, sg_done, b)
                after(pool, GT_done, b, 1)
                pool.tensor_tensor(gs[:, :], gc[:, :], sg[:, :], ALU.mult).then_inc(gs_done, 1)

            def gate_rows(b):
                if b == 0:
                    pool.wait_ge(row_done, 4)
                after(pool, prob_done, b)
                pool.tensor_tensor(rows[:, b, :, C_GP:C_GP + D],
                                   gb_row[:, b, :].unsqueeze(1).to_broadcast([P, NJ, D]),
                                   prob[:, :].unsqueeze(2).to_broadcast([P, NJ, D]), ALU.mult
                                   ).then_inc(gp_done, 1)

            def scatter(b):
                if b == 0:
                    pool.wait_ge(blank_out, 16 * NPAIR)
                pool.wait_ge(gp_done, b + 1)
                after(pool, h2_done, b)
                after(pool, slot_done, b)
                for j in range(NJ):
                    pool.indirect_dma_start(
                        out=disp_d, out_offset=bass.IndirectOffsetOnAxis(ap=slot[:, b, j:j + 1], axis=0),
                        in_=rows[:, b, j, :], in_offset=None, bounds_check=NSLOT - 1,
                        oob_is_err=False).then_inc(scattered, 16)

            batches([
                (3, silu), (2, log_denominator), (0, squares), (5, gate_rows),
                (1, pair_sums), (5, scatter)])

            pool.wait_ge(x1_out, 16 * NB)

            last_token = pool.to_reg(NTOK - 1)

            def send(i, par, k):
                after(pool, fin_done, i)
                carry_waits(pool, pool_past)
                for n in range(NS):
                    pool.indirect_dma_start(
                        out=out_d.rearrange("b t d -> (b t) d"),
                        out_offset=bass.IndirectOffsetOnAxis(
                            ap=rest[par][:, n, C_TOK - D:C_TOK - D + 1].bitcast(i32), axis=0),
                        in_=fin[par][:, n, :], in_offset=None, bounds_check=last_token,
                        oob_is_err=False).then_inc(final_out[par], 16)

            in_pairs(pool, send)

        @block.scalar
        def _(act):
            act.preload_act_table_set("natural_log_exp_and_others")
            def ln1_scale(b):
                after(act, ln1_mv, b)
                act.activation(ln1[:, :], mv1[:, :, 1], ACT.Ln, bias=eps[:, 0:1]).then_inc(ln1_ln, 1)
                act.wait_ge(ln1_ln, b + 1)
                after(act, xh_done, b, 1)
                act.activation(rs1[:, :], ln1[:, :], ACT.Exp, scale=-0.5).then_inc(ln1_rs, 1)

            def modulate1(b):
                after(act, xhT_ps, b)
                after(act, x1_ps, b, NHT)
                if b == 0:
                    act.wait_ge(mod_done, 1)
                act.activation(hT[b % NHT][:, :], ps_t, ACT.Identity, bias=mod[:, SA, b:b + 1],
                               scale=mod[:, CA, b:b + 1]).then_inc(hT_done, 1)

            def square_sums(b):
                after(act, qk_ps, b)
                after(act, nrm_b, b, 1)
                for j in range(NJ):
                    for m in range(2):
                        last = act.activation(junk[:, 2 * j + m, :], ps_qk[:, j, m * D:(m + 1) * D],
                                              ACT.Square, accum_out=ssq[:, j, m:m + 1])
                last.then_inc(ssq_done, 1)

            def rms_scales(b):
                after(act, nrm_b, b)
                act.activation(nrl[:, :], nrm[:, :], ACT.Ln).then_inc(nrl_done, 1)
                act.wait_ge(nrl_done, b + 1)
                after(act, kv_done, b, 1)
                act.activation(nrr[:, :], nrl[:, :], ACT.Exp, scale=-0.5).then_inc(nrr_done, 1)

            def exp_qk(b):
                after(act, qkn_done, b)
                after(act, sumkv_ps, b, 2)
                after(act, eqT_ps, b, 2)
                act.activation(ewkv[b % 2][:, 0:NJ, 0:2, :].rearrange("p j m d -> p j (m d)"),
                               qkn[:, :, :].rearrange("p (j m) d -> p j (m d)", m=2),
                               ACT.Exp).then_inc(ew_done, 1)

            def log_q(b):
                after(act, eqT_ps, b)
                after(act, lden_done, b, 1)
                act.activation(lq[:, :], ps_g, ACT.Ln, bias=eps[:, 2:3]).then_inc(lq_done, 1)

            def log_w(b):
                after(act, sumw_ps, b)
                after(act, lden_done, b, 1)
                act.activation(lw[:, :], ps_w, ACT.Ln, bias=eps[:, 1:2]).then_inc(lw_done, 1)

            def reciprocal(b):
                after(act, lden_done, b)
                after(act, yT_done, b, 1)
                act.activation(rden[:, :], lden[:, :], ACT.Exp, scale=-1.0).then_inc(rden_done, 1)

            def exp_g(b):
                after(act, gc_done, b)
                act.activation(eg[:, :], gc[:, :], ACT.Exp, scale=-1.0).then_inc(eg_done, 1)

            def log_g(b):
                act.wait_ge(eg_done, b + 1)
                act.activation(lg[:, :], eg[:, :], ACT.Ln, bias=eps[:, 2:3]).then_inc(lg_done, 1)

            def sigmoid_g(b):
                act.wait_ge(lg_done, b + 1)
                after(act, gs_done, b, 1)
                act.activation(sg[:, :], lg[:, :], ACT.Exp, scale=-1.0).then_inc(sg_done, 1)

            def ln2_scale(b):
                after(act, ln2_mv, b)
                act.activation(ln2[:, :], mv2[:, :, 1], ACT.Ln, bias=eps[:, 0:1]).then_inc(ln2_ln, 1)
                act.wait_ge(ln2_ln, b + 1)
                act.activation(rs2[:, :], ln2[:, :], ACT.Exp, scale=-0.5).then_inc(ln2_rs, 1)

            def normalize2(b):
                after(act, nm2_done, b)
                after(act, xh2T_ps, b, 1)
                for j in range(NJ):
                    last = act.activation(xh2[:, j, :], rows[:, b, j, C_X1:C_X1 + D], ACT.Identity,
                                          bias=nm2[:, j:j + 1], scale=rs2[:, j:j + 1])
                last.then_inc(xh2_done, 1)

            def modulate2(b):
                after(act, xh2T_ps, b)
                after(act, h2_ps, b, 1)
                act.activation(h2T[:, :], ps_t, ACT.Identity, bias=mod[:, SB, b:b + 1],
                               scale=mod[:, CB, b:b + 1]).then_inc(h2T_done, 1)

            def h2_rows(b):
                after(act, h2_ps, b)
                act.copy(rows[:, b, :, 0:D], ps_g.rearrange("p (j d) -> p j d", d=D)).then_inc(h2_done, 1)

            def exp_logits(b):
                after(act, dl_done, b)
                after(act, psm_done, b, 1)
                act.activation(pe_[:, :, :], dl[:, :, :], ACT.Exp).then_inc(pe_done, 1)

            act.wait_ge(c_in, 32)
            act.activation(c_e[:, :], c_sb[:, :], ACT.Exp, scale=-1.0).then_inc(c_step, 1)
            ln1_scale(0)
            act.wait_ge(wt_ps, 1)
            act.mul(wqkvT[:, 0:D], bank01[:, 0:D], -1.0)
            act.copy(wqkvT[:, D:3 * D], bank01[:, D:3 * D])
            act.copy(wswT[:, :], bank01[:, 512:512 + 2 * D])
            act.copy(gwT[:, :], bank01[:, 512 + 2 * D:512 + 2 * D + NE]).then_inc(wt_done, 1)

            def copy_rows():
                for n, (dst, src) in enumerate(((gb_row, ps_g), (woga, ps_w), (woga, ps_kv), (gb_row, ps_u))):
                    act.wait_ge(row_ps, n + 1)
                    half = n // 2
                    act.copy(dst[:, 4 * half:4 * half + 4, :], src.rearrange("p (b d) -> p b d", d=D)
                             ).then_inc(row_done, 1)

            batches([
                (5, normalize2), (3, reciprocal), (0, ln1_scale), (2, log_q),
                (1, square_sums), (5, modulate2), (3, exp_g), (1, rms_scales), (3, log_g),
                (2, log_w), (3, sigmoid_g), (0, modulate1), (4, ln2_scale), (5, h2_rows),
                (5, exp_logits), (1, exp_qk)], early=(ln1_scale,), then=copy_rows)

            HB = 3

            def experts(i, par, k):
                for c in range(2 * NF):
                    e, f = c // NF, c % NF
                    act.wait_ge(h_ps, 2 * NF * i + c + 1)
                    if f == 0 and (not isinstance(i, int) or i >= 1):
                        act.wait_ge(o_ps, 2 * i - 1 + e)
                    act.activation(HT[e][:, f, :], ps_h[c % HB][:, 0:CAP], ACT.Gelu_apprx_tanh
                                   ).then_inc(h_done, 1)

            in_pairs(act, experts)

        @block.vector
        def _(dve):
            def stats1(b):
                dve.wait_ge(x_in[b], 16)
                for j in range(NJ):
                    last = dve.bn_stats(st1[:, j, :], x_all[:, b, j, :])
                last.then_inc(ln1_st, 1)

            def aggregate1(b):
                dve.wait_ge(ln1_st, b + 1)
                after(dve, ln1_ln, b, 1)
                for j in range(NJ):
                    last = dve.bn_aggr(mv1[:, j, :], st1[:, j, :])
                last.then_inc(ln1_mv, 1)

            def normalize1(b):
                after(dve, ln1_rs, b)
                after(dve, xhT_ps, b, 1)
                for j in range(NJ):
                    last = dve.tensor_scalar(xh[:, j, :], x_all[:, b, j, :], mv1[:, j, 0:1],
                                             rs1[:, j:j + 1], ALU.subtract, ALU.mult)
                last.then_inc(xh_done, 1)

            def h_means(b):
                after(dve, mh_ps, b)
                after(dve, nrl_done, b, 1)
                dve.tensor_scalar(nrm[:, 2 * NJ:3 * NJ], ps_mh, 1.0 / D, EPS_RMS, ALU.mult, ALU.add
                                  ).then_inc(mh_done, 1)
                dve.wait_ge(mh_done, b + 1)
                dve.tensor_scalar(mh[:, :], nrm[:, 2 * NJ:3 * NJ], EPS_RMS, None, ALU.mult
                                  ).then_inc(nrm_a, 1)

            def qk_means(b):
                after(dve, ssq_done, b)
                dve.wait_ge(nrm_a, b + 1)
                dve.scalar_tensor_tensor(nrm[:, 0:2 * NJ].rearrange("p (j m) -> p j m", m=2), ssq[:, :, :],
                                         1.0 / D, mh[:, :].unsqueeze(2).to_broadcast([P, NJ, 2]),
                                         ALU.mult, ALU.add).then_inc(nrm_b, 1)

            def normalize_qk(b):
                after(dve, nrr_done, b)
                after(dve, qk_ps, b)
                after(dve, ssq_done, b)
                after(dve, ew_done, b, 1)
                dve.tensor_tensor(qkn[:, :, :], ps_qk.rearrange("p j (m d) -> p (j m) d", m=2),
                                  nrr[:, 0:2 * NJ].unsqueeze(2).to_broadcast([P, 2 * NJ, D]), ALU.mult
                                  ).then_inc(qkn_done, 1)

            def weigh_v(b):
                after(dve, v_ps, b)
                after(dve, ew_done, b)
                t = ewkv[b % 2]
                for j in range(NJ):
                    last = dve.scalar_tensor_tensor(t[:, j, 2, :], ps_v[:, j, :],
                                                    nrr[:, 2 * NJ + j:2 * NJ + j + 1],
                                                    t[:, j, 1, :], ALU.mult, ALU.mult)
                last.then_inc(kv_done, 1)

            def divide(b):
                after(dve, rden_done, b)
                after(dve, sumkv_ps, b)
                after(dve, u_ps, b, 1)
                dve.tensor_tensor(yT[:, :], ps_kv, rden[:, :], ALU.mult).then_inc(yT_done, 1)

            def clamp_g(b):
                after(dve, g_ps, b)
                after(dve, gs_done, b, 1)
                dve.tensor_scalar(gc[:, :], ps_g, -43.0, None, ALU.max).then_inc(gc_done, 1)

            def gate_u(b):
                after(dve, gs_done, b)
                after(dve, u_ps, b)
                after(dve, x1_ps, b, 2)
                dve.tensor_tensor(GT[b % 2][:, :], gs[:, :], ps_u, ALU.mult).then_inc(GT_done, 1)

            def residual(b):
                after(dve, x1_ps, b)
                dve.tensor_tensor(rows[:, b, :, C_X1:C_X1 + D], x_all[:, b, :, :],
                                  ps_u.rearrange("p (j d) -> p j d", d=D), ALU.add).then_inc(x1_done, 1)

            def stats2(b):
                dve.wait_ge(x1_done, b + 1)
                for j in range(NJ):
                    last = dve.bn_stats(st2[:, j, :], rows[:, b, j, C_X1:C_X1 + D])
                last.then_inc(ln2_st, 1)

            def aggregate2(b):
                dve.wait_ge(ln2_st, b + 1)
                after(dve, ln2_ln, b, 1)
                for j in range(NJ):
                    last = dve.bn_aggr(mv2[:, j, :], st2[:, j, :])
                last.then_inc(ln2_mv, 1)

            def shift2(b):
                after(dve, ln2_rs, b)
                after(dve, xh2_done, b, 1)
                dve.scalar_tensor_tensor(nm2[:, :], mv2[:, :, 0], -1.0, rs2[:, :], ALU.mult, ALU.mult
                                         ).then_inc(nm2_done, 1)

            def top1(b):
                after(dve, logit_ps, b)
                lg_v = ps_logit.rearrange("p (j e) -> p j e", e=NE)
                dve.tensor_reduce(mx[:, :], lg_v, X, ALU.max).then_inc(mx_done, 1)
                dve.wait_ge(mx_done, b + 1)
                after(dve, pe_done, b, 1)
                dve.tensor_tensor(dl[:, :, :], lg_v, mx[:, :].unsqueeze(2).to_broadcast([P, NJ, NE]),
                                  ALU.subtract).then_inc(dl_done, 1)
                dve.wait_ge(dl_done, b + 1)
                dve.scalar_tensor_tensor(cand[:, :, :], dl[:, :, :], 0.0, rev[:, :, :], ALU.is_ge, ALU.mult
                                         ).then_inc(cand_done, 1)
                dve.wait_ge(cand_done, b + 1)
                dve.tensor_reduce(best[:, b, :], cand[:, :, :], X, ALU.max).then_inc(best_done, 1)
                dve.wait_ge(best_done, b + 1)
                dve.tensor_tensor(oh[b % 2][:, :, :], rev[:, :, :],
                                  best[:, b, :].unsqueeze(2).to_broadcast([P, NJ, NE]),
                                  ALU.is_equal).then_inc(oh_done, 1)

            def top_prob(b):
                after(dve, pe_done, b)
                dve.tensor_reduce(psm[:, :], pe_[:, :, :], X, ALU.add).then_inc(psm_done, 1)
                dve.wait_ge(psm_done, b + 1)
                after(dve, gp_done, b, 1)
                dve.reciprocal(prob[:, :], psm[:, :]).then_inc(prob_done, 1)

            def slots(b):
                dve.wait_ge(oh_done, b + 1)
                dve.tensor_reduce(ohs[:, :], oh[b % 2][:, :, :].rearrange("p j e -> p e j"), X, ALU.add
                                  ).then_inc(ohs_done, 1)
                after(dve, rank_ps, b)
                dve.tensor_tensor(rk[:, :, :], oh[b % 2][:, :, :],
                                  ps_rank.rearrange("p (j e) -> p j e", e=NE), ALU.mult
                                  ).then_inc(rk_done, 1)
                dve.wait_ge(ohs_done, b + 1)
                dve.tensor_tensor(seen[:, :], seen[:, :], ohs[:, :], ALU.add).then_inc(seen_done, 1)
                dve.wait_ge(rk_done, b + 1)
                dve.tensor_reduce(rank[:, :], rk[:, :, :], X, ALU.add).then_inc(rank_done, 1)
                dve.wait_ge(rank_done, b + 1)
                dve.scalar_tensor_tensor(sl_a[:, :], best[:, b, :], -float(CAP), rank[:, :], ALU.mult, ALU.add)
                dve.tensor_scalar(sl_o[:, :], rank[:, :], float(CAP), float(NOWHERE), ALU.is_gt, ALU.mult
                                  ).then_inc(sl_done, 1)
                dve.wait_ge(sl_done, b + 1)
                dve.scalar_tensor_tensor(slot[:, b, :], sl_a[:, :], float(NE * CAP - 1), sl_o[:, :],
                                         ALU.add, ALU.add).then_inc(slot_done, 1)

            dve.memset(eps[:, 0:1], EPS_LN)
            dve.memset(eps[:, 1:2], 1e-06)
            dve.memset(eps[:, 2:4], 1.0).then_inc(mod_step, 1)
            dve.wait_ge(c_step, 1)
            dve.tensor_scalar(c_e[:, :], c_e[:, :], 1.0, None, ALU.add).then_inc(c_step, 1)
            dve.wait_ge(c_step, 2)
            dve.reciprocal(c_e[:, :], c_e[:, :]).then_inc(c_step, 1)
            dve.wait_ge(c_step, 3)
            dve.tensor_tensor(c_s[:, :], c_sb[:, :], c_e[:, :], ALU.mult).then_inc(c_step, 1)
            dve.wait_ge(mod_ps, 1)
            dve.tensor_copy(c_T[:, :], bank3[:, 0:NB]).then_inc(c_step, 1)
            stats1(0)
            aggregate1(0)
            normalize1(0)
            dve.wait_ge(mod_ps, 2)
            dve.tensor_copy(mod_r[:, :, :], bank3[:, 64:64 + 6 * NB].rearrange("p (m b) -> p m b", m=6)
                            ).then_inc(mod_step, 1)
            dve.wait_ge(mod_step, 2)
            for n, m in enumerate((GA, GB)):
                dve.tensor_scalar(sgn[:, n, :], mod_r[:, m, :], 0.0, 2.0, ALU.is_ge, ALU.mult)
                dve.tensor_scalar(mod[:, m, :], mod_r[:, m, :], -1.0, None, ALU.mult)
            for m in (CA, CB):
                dve.tensor_scalar(mod[:, m, :], mod_r[:, m, :], 1.0, None, ALU.add)
            dve.tensor_copy(mod[:, SA, :], mod_r[:, SA, :])
            dve.tensor_copy(mod[:, SB, :], mod_r[:, SB, :]).then_inc(mod_step, 1)
            dve.wait_ge(mod_step, 3)
            for m in (GA, GB):
                last = dve.tensor_tensor(mod[:, m, :], mod[:, m, :], mod_r[:, m, :], ALU.max)
            last.then_inc(mod_step, 1)
            dve.wait_ge(mod_step, 4)
            for m in (GA, GB):
                last = dve.tensor_scalar(mod[:, m, :], mod[:, m, :], 0.25, None, ALU.max)
            last.then_inc(mod_step, 1)
            dve.wait_ge(mod_step, 5)
            for n, m in enumerate((GA, GB)):
                last = dve.scalar_tensor_tensor(mod[:, m, :], sgn[:, n, :], -1.0, mod[:, m, :],
                                                ALU.add, ALU.mult)
            last.then_inc(mod_done, 1)

            def diagonals():
                dve.wait_ge(mod_done, 1)
                for dst, m in ((diag_ga, GA), (diag_gb, GB)):
                    dve.tensor_tensor(dst[:, :, :], ident[:, :].unsqueeze(1).to_broadcast([P, NB, D]),
                                      mod[:, m, :].unsqueeze(2).to_broadcast([P, NB, D]), ALU.mult
                                      ).then_inc(diag_done, 1)

            dve.wait_ge(consts, 4)
            batches([
                (0, stats1), (0, aggregate1), (2, weigh_v), (3, divide), (0, normalize1),
                (1, h_means), (3, clamp_g), (4, residual), (1, qk_means), (4, stats2),
                (1, normalize_qk), (4, aggregate2), (5, top1), (4, shift2), (3, gate_u),
                (5, top_prob), (5, slots)], early=(stats1, aggregate1, normalize1), then=diagonals)

            def xt_copy(i, par):
                after(dve, xt_ps, i)
                if not isinstance(i, int) or i >= 2:
                    dve.wait_ge(h_ps, 2 * NF * (i - 1))
                dve.tensor_copy(XT[par][:, :], ps_xt).then_inc(xt_done, 1)

            def combine(i, par, k):
                after(dve, y_ps, i)
                dve.wait_ge(rest_in[par], 16 * (k + 1))
                after(dve, fin_done, i, 1)
                dve.tensor_tensor(yw[:, :, :], ps_y.rearrange("p (n d) -> p n d", d=D),
                                  rest[par][:, :, C_GP - D:C_GP], ALU.mult).then_inc(yw_done, 1)
                dve.wait_ge(yw_done, i + 1)
                if not isinstance(i, int) or i >= 2:
                    dve.wait_ge(final_out[par], 16 * NS * k)
                dve.tensor_tensor(fin[par][:, :, :], yw[:, :, :], rest[par][:, :, C_X1 - D:C_X1],
                                  ALU.add).then_inc(fin_done, 1)

            def experts(i, par, k):
                if not isinstance(i, int) or i >= 1:
                    combine(i - 1, 1 - par, k - 1 + par)
                for e in range(2):
                    dve.wait_ge(o_ps, 2 * i + e + 1)
                    if e == 0:
                        after(dve, y_ps, i, 1)
                    dve.tensor_copy(OT[:, e * CAP:(e + 1) * CAP], ps_o).then_inc(o_done, 1)
                    if e == 0 and not (isinstance(i, int) and i == NPAIR - 1):
                        xt_copy(i + 1, 1 - par)

            xt_copy(0, 0)
            in_pairs(dve, experts)
            combine(NPAIR - 1, 1, NPAIR // 2 - 1)

        @block.tensor
        def _(pe):
            def transpose1(b):
                after(pe, xh_done, b)
                claim(pe, "t", hT_done, b)
                for j in range(NJ):
                    last = pe.transpose(ps_t[:, j * P:(j + 1) * P], xh[:, j, :], ident[:, :])
                last.then_inc(xhT_ps, 1)

            def h_square_sums(b):
                after(pe, hsq_done, b)
                claim(pe, "v", mh_done, b)
                for j in range(NJ):
                    last = pe.matmul(ps_mh[:, j:j + 1], hsq[:, j * P:(j + 1) * P], tri[:, P:P + 1],
                                     start=True, stop=True)
                last.then_inc(mh_ps, 1)

            def project_qk(b):
                after(pe, hT_done, b)
                claim(pe, "qk", qkn_done, b)
                for j in range(NJ):
                    last = pe.matmul(ps_qk[:, j, :], hT[b % NHT][:, j * P:(j + 1) * P], wqkvT[:, 0:2 * D],
                                     start=True, stop=True)
                last.then_inc(qk_ps, 1)

            def project_v(b):
                after(pe, hT_done, b)
                claim(pe, "v", kv_done, b)
                for j in range(NJ):
                    last = pe.matmul(ps_v[:, j, :], hT[b % NHT][:, j * P:(j + 1) * P],
                                     wqkvT[:, 2 * D:3 * D], start=True, stop=True)
                last.then_inc(v_ps, 1)

            def transpose_q(b):
                after(pe, ew_done, b)
                claim(pe, "g", lq_done, b)
                for j in range(NJ):
                    last = pe.transpose(ps_g[:, j * P:(j + 1) * P], ewkv[b % 2][:, j, 0, :], ident[:, :])
                last.then_inc(eqT_ps, 1)

            def running_sum(ps, t, m):
                pe.matmul(ps[:, 0:2 * P], t[:, 0, m, :], tri[:, 0:2 * P], start=True, stop=False)
                pe.matmul(ps[:, P:2 * P], t[:, 1, m, :], tri[:, 0:P], start=False, stop=False)
                pe.matmul(ps[:, 2 * P:4 * P], t[:, NJ, m, :], tri[:, P:3 * P], start=False, stop=False)
                pe.matmul(ps[:, 2 * P:4 * P], t[:, 2, m, :], tri[:, 0:2 * P], start=False, stop=False)
                return pe.matmul(ps[:, 3 * P:4 * P], t[:, 3, m, :], tri[:, 0:P], start=False, stop=True)

            def sum_w(b):
                after(pe, pair_done, b)
                claim(pe, "w", lw_done, b)
                running_sum(ps_w, ewkv[b % 2], 1).then_inc(sumw_ps, 1)

            def sum_kv(b):
                after(pe, pair_done, b)
                claim(pe, "kv", yT_done, b)
                running_sum(ps_kv, ewkv[b % 2], 2).then_inc(sumkv_ps, 1)

            def project_g(b):
                after(pe, yT_done, b)
                claim(pe, "g", gc_done, b)
                pe.matmul(ps_g, wswT[:, D:2 * D], yT[:, :], start=True, stop=True).then_inc(g_ps, 1)

            def project_u(b):
                after(pe, yT_done, b)
                claim(pe, "u", GT_done, b)
                pe.matmul(ps_u, wswT[:, 0:D], yT[:, :], start=True, stop=True).then_inc(u_ps, 1)

            def project_out(b):
                after(pe, GT_done, b)
                claim(pe, "u", x1_done, b)
                for j in range(NJ):
                    pe.matmul(ps_u[:, j * P:(j + 1) * P], hT[b % NHT][:, j * P:(j + 1) * P],
                              diag_ga[:, b, :], start=True, stop=False)
                    last = pe.matmul(ps_u[:, j * P:(j + 1) * P], GT[b % 2][:, j * P:(j + 1) * P],
                                     woga[:, b, :], start=False, stop=True)
                last.then_inc(x1_ps, 1)

            def transpose2(b):
                after(pe, xh2_done, b)
                claim(pe, "t", h2T_done, b)
                for j in range(NJ):
                    last = pe.transpose(ps_t[:, j * P:(j + 1) * P], xh2[:, j, :], ident[:, :])
                last.then_inc(xh2T_ps, 1)

            def logits(b):
                after(pe, h2T_done, b)
                claim(pe, "w", dl_done, b)
                for j in range(NJ):
                    last = pe.matmul(ps_logit[:, j * NE:(j + 1) * NE], h2T[:, j * P:(j + 1) * P], gwT[:, :],
                                     start=True, stop=True)
                last.then_inc(logit_ps, 1)

            def h2_back(b):
                after(pe, h2T_done, b)
                claim(pe, "g", h2_done, b)
                for j in range(NJ):
                    last = pe.transpose(ps_g[:, j * P:(j + 1) * P], h2T[:, j * P:(j + 1) * P], ident[:, :])
                last.then_inc(h2_ps, 1)

            def ranks(b):
                after(pe, oh_done, b)
                after(pe, seen_done, b, 1)
                claim(pe, "t", rk_done, b)
                hot = oh[b % 2]
                pe.matmul(ps_rank, ones_b[:, :], seen[:, :].unsqueeze(1).to_broadcast([P, NJ, NE]),
                          start=True, stop=False)
                pe.matmul(ps_rank, tri_b[:, :], hot[:, :, :].rearrange("p j e -> p (j e)"),
                          start=False, stop=False)
                for j in range(NJ - 1):
                    last = pe.matmul(ps_rank[:, (j + 1) * NE:NJ * NE], ones_b[:, :],
                                     hot[:, j, :].unsqueeze(1).to_broadcast([P, NJ - 1 - j, NE]),
                                     start=False, stop=(j == NJ - 2))
                last.then_inc(rank_ps, 1)

            pe.wait_ge(consts, 4)
            pe.wait_ge(w_in, 64)
            for m in range(3):
                pe.transpose(bank01[:, m * D:(m + 1) * D], wqkv[:, m, :], ident[:, :])
            for m in range(2):
                pe.transpose(bank01[:, 512 + m * D:512 + (m + 1) * D], wsw[:, m, :], ident[:, :])
            pe.transpose(bank01[:, 512 + 2 * D:512 + 2 * D + NE], gw[:, :], ident[0:NE, 0:NE]
                         ).then_inc(wt_ps, 1)
            pe.wait_ge(c_step, 4)
            pe.transpose(bank3[:, 0:NB], c_s[:, :], ident[0:NB, 0:NB]).then_inc(mod_ps, 1)
            pe.wait_ge(c_step, 5)
            for m in range(6):
                last = pe.matmul(bank3[:, 64 + m * NB:64 + (m + 1) * NB], wmod[:, m, :], c_T[:, :],
                                 start=True, stop=True)
            last.then_inc(mod_ps, 1)
            transpose1(0)
            pe.wait_ge(wt_done, 1)

            def row_products():
                pe.wait_ge(diag_done, 2)
                for lhsT, diag, half, dst in ((tri[:, P:2 * P], diag_gb, 0, ps_g), (wout[:, :], diag_ga, 0, ps_w),
                                              (wout[:, :], diag_ga, 1, ps_kv),
                                              (tri[:, P:2 * P], diag_gb, 1, ps_u)):
                    pe.matmul(dst, lhsT, diag[:, 4 * half:4 * half + 4, :].rearrange("p b d -> p (b d)"),
                              start=True, stop=True).then_inc(row_ps, 1)

            batches([
                (5, transpose2), (1, h_square_sums), (3, project_g), (2, sum_w),
                (0, transpose1), (2, sum_kv), (5, logits), (5, h2_back), (3, project_u),
                (1, project_v), (5, ranks), (0, project_qk), (1, transpose_q),
                (3, project_out)], early=(transpose1,), then=row_products)

            HB = 3

            def xt(i, par, k):
                pe.wait_ge(hin_in[par], 16 * (k + 1))
                after(pe, xt_done, i, 1)
                for n in range(NS):
                    last = pe.transpose(ps_xt[:, n * P:(n + 1) * P], hin[par][:, n, :], ident[:, :])
                last.then_inc(xt_ps, 1)

            def rows_back(i):
                pe.wait_ge(o_done, 2 * i + 2)
                after(pe, yw_done, i, 1)
                for n in range(NS):
                    last = pe.transpose(ps_y[:, n * P:(n + 1) * P], OT[:, n * P:(n + 1) * P], ident[:, :])
                last.then_inc(y_ps, 1)

            def experts(i, par, k):
                first = isinstance(i, int) and i == 0
                after(pe, xt_done, i)
                pe.wait_ge(wts_in[par], 32 * (k + 1))
                for c in range(2 * NF):
                    e, f = c // NF, c % NF
                    if c >= HB:
                        pe.wait_ge(h_done, 2 * NF * i + c - HB + 1)
                    elif not first:
                        back = max(q for q in range(2 * NF) if q % HB == c)
                        pe.wait_ge(h_done, 2 * NF * i + (back - 2 * NF + 1))
                    pe.matmul(ps_h[c % HB][:, 0:CAP], w1[par][:, e, f:FF:NF],
                              XT[par][:, e * CAP:(e + 1) * CAP], start=True, stop=True).then_inc(h_ps, 1)
                    if c == NF - 1 and not first:
                        rows_back(i - 1)
                for e in range(2):
                    pe.wait_ge(h_done, 2 * NF * i + (e + 1) * NF)
                    if e == 1 or not first:
                        pe.wait_ge(o_done, 2 * i + e)
                    for f in range(NF):
                        last = pe.matmul(ps_o, w2[par][:, e, f, :], HT[e][:, f, :],
                                         start=(f == 0), stop=(f == NF - 1))
                    last.then_inc(o_ps, 1)
                    if e == 0 and not (isinstance(i, int) and i == NPAIR - 1):
                        xt(i + 1, 1 - par, k + par)

            xt(0, 0, 0)
            in_pairs(pe, experts)
            rows_back(NPAIR - 1)


_INS = ['L0_attn_x', 'L0_attn_w_qkv', 'L0_attn_w_swiglu', 'L0_attn_w_out', 'L0_ffn_gate_w', 'L0_ffn_w1',
        'L0_ffn_w2', 'L0_c', 'L0_wmod']
_OUTS = [((8, 512, 128), 'float32')]


def kernel(**inputs):
    import numpy as _np
    import concourse.bacc as _bacc
    from concourse import mybir as _mybir
    from concourse.bass_utils import run_bass_kernel_spmd as _run

    nc = _bacc.Bacc("TRN2", target_bir_lowering=False, num_devices=1)
    arrays, args = {}, []
    for name in _INS:
        a = _np.ascontiguousarray(inputs[name])
        arrays[f"in_{name}_dram"] = a
        args.append(nc.dram_tensor(f"in_{name}_dram", a.shape, _mybir.dt.from_np(a.dtype), kind="ExternalInput").ap())
    for i, (shape, dtype) in enumerate(_OUTS):
        dt = _mybir.dt.from_np(_np.dtype(dtype))
        args.append(nc.dram_tensor(f"out_{i}_dram", shape, dt, kind="ExternalOutput").ap())
    adaln_attention_moe(nc, *args)
    r = _run(nc, [arrays], core_ids=[0])
    got = tuple(r.results[0][f"out_{i}_dram"] for i in range(len(_OUTS)))
    return got[0]
```

```python
import concourse.bass as bass
from concourse import mybir
from contextlib import ExitStack


def adaln_attention_moe(
    nc: bass.Bass,
    x_d: bass.AP,
    w_qkv_d: bass.AP,
    w_swiglu_d: bass.AP,
    w_out_d: bass.AP,
    gate_w_d: bass.AP,
    w1_d: bass.AP,
    w2_d: bass.AP,
    c_d: bass.AP,
    wmod_d: bass.AP,
    out_d: bass.AP,
):
    f32 = mybir.dt.float32
    f32r = mybir.dt.float32r
    bf16 = mybir.dt.bfloat16
    i32 = mybir.dt.int32
    ALU = mybir.AluOpType
    ACT = mybir.ActivationFunctionType
    X = mybir.AxisListType.X

    P = 128
    NB, T, D = x_d.shape
    NJ = T // P
    NTOK = NB * T
    NE, _, FF = w1_d.shape
    NF = FF // P
    CAP = int(1.25 * NTOK / NE)
    CAP += CAP % 2
    NSLOT = NE * CAP
    NPAIR = NE // 2
    PS = 2 * CAP
    NS = PS // P
    EPS_RMS = 1.1920929e-07
    EPS_LN = 1e-05
    NOWHERE = 1 << 20
    C_X1, C_GP, C_TOK, ROW = D, 2 * D, 3 * D, 3 * D + 2
    SA, CA, GA, SB, CB, GB = range(6)

    disp_d = nc.dram_tensor("dispatched_rows", [NSLOT, ROW], f32, kind="Internal").ap()

    ctx = ExitStack()
    with ctx:
        def sb(name, shape, dt=f32):
            return ctx.enter_context(nc.sbuf_tensor(name, shape, dt))

        def sem(name):
            return ctx.enter_context(nc.semaphore(name))

        bank01 = ctx.enter_context(nc.psum_tensor("bank01", [P, 1024], f32))
        bank67 = ctx.enter_context(nc.psum_tensor("bank67", [P, 1024], f32))
        bank2, bank3, bank4, bank5 = [
            ctx.enter_context(nc.psum_tensor(f"bank{n}", [P, 512], f32)) for n in (2, 3, 4, 5)]
        ps_qk = bank01[:, :].rearrange("p (j c) -> p j c", j=NJ)
        ps_t = bank2[:, :]
        ps_rank = bank2[:, 0:NJ * NE]
        ps_v = bank3[:, :].rearrange("p (j c) -> p j c", j=NJ)
        ps_mh = bank3[:, 0:NJ]
        ps_w = bank4[:, :]
        ps_logit = bank4[:, 0:NJ * NE]
        ps_kv = bank5[:, :]
        ps_u = bank67[:, 0:512]
        ps_g = bank67[:, 512:1024]
        ps_xt = bank01[:, 0:PS]
        ps_y = bank67[:, 0:PS]
        ps_h = [bank2, bank3, bank4]
        ps_o = bank5[:, 0:CAP]

        ident = sb("ident", [P, P])
        tri = sb("tri", [P, T])
        tri_b = sb("tri_b", [P, P], bf16)
        ones_b = sb("ones_b", [P, P], bf16)
        eps = sb("eps", [P, 4])
        rev_i = sb("rev_i", [P, NJ * NE], i32)
        rev = sb("rev", [P, NJ, NE])
        tokid = sb("tokid", [P, NTOK // P], i32)
        blank = sb("blank", [P, ROW])

        c_sb = sb("c_sb", [NB, D])
        c_e = sb("c_e", [NB, D])
        c_s = sb("c_s", [NB, D])
        c_T = sb("c_T", [P, NB])
        wmod = sb("wmod", [P, 6, D])
        mod = sb("mod", [P, 6, NB])
        mod_r = sb("mod_r", [P, 6, NB])
        sgn = sb("sgn", [P, 2, NB])
        wqkv = sb("wqkv", [P, 3, D])
        wqkvT = sb("wqkvT", [P, 3 * D])
        wsw = sb("wsw", [P, 2, D])
        wswT = sb("wswT", [P, 2 * D])
        wout = sb("wout", [P, D])
        gw = sb("gw", [NE, D])
        gwT = sb("gwT", [P, NE])
        diag_ga = sb("diag_ga", [P, NB, D])
        diag_gb = sb("diag_gb", [P, NB, D])
        woga = sb("woga", [P, NB, D])
        gb_row = sb("gb_row", [P, NB, D])

        x_all = sb("x_all", [P, NB, NJ, D])
        st1 = sb("st1", [P, NJ, 6])
        mv1 = sb("mv1", [P, NJ, 2])
        ln1 = sb("ln1", [P, NJ])
        rs1 = sb("rs1", [P, NJ])
        xh = sb("xh", [P, NJ, D])
        NHT = 5
        hT = [sb(f"hT{n}", [P, T]) for n in range(NHT)]
        hsq = sb("hsq", [P, T])
        ssq = sb("ssq", [P, NJ, 2])
        junk = sb("junk", [P, 2 * NJ, D])
        mh = sb("mh", [P, NJ])
        nrm = sb("nrm", [P, 3 * NJ])
        nrl = sb("nrl", [P, 3 * NJ])
        nrr = sb("nrr", [P, 3 * NJ])
        qkn = sb("qkn", [P, 2 * NJ, D])
        ewkv = [sb(f"ewkv{n}", [P, NJ + 1, 3, D]) for n in range(2)]
        lq = sb("lq", [P, T])
        lw = sb("lw", [P, T])
        lden = sb("lden", [P, T])
        rden = sb("rden", [P, T])
        yT = sb("yT", [P, T])
        gc = sb("gc", [P, T])
        eg = sb("eg", [P, T])
        lg = sb("lg", [P, T])
        sg = sb("sg", [P, T])
        gs = sb("gs", [P, T])
        GT = [sb(f"GT{n}", [P, T]) for n in range(2)]
        st2 = sb("st2", [P, NJ, 6])
        mv2 = sb("mv2", [P, NJ, 2])
        ln2 = sb("ln2", [P, NJ])
        rs2 = sb("rs2", [P, NJ])
        nm2 = sb("nm2", [P, NJ])
        xh2 = sb("xh2", [P, NJ, D])
        h2T = sb("h2T", [P, T])
        mx = sb("mx", [P, NJ])
        dl = sb("dl", [P, NJ, NE])
        pe_ = sb("pe_", [P, NJ, NE])
        psm = sb("psm", [P, NJ])
        prob = sb("prob", [P, NJ])
        cand = sb("cand", [P, NJ, NE])
        best = sb("best", [P, NB, NJ])
        oh = [sb(f"oh{n}", [P, NJ, NE], bf16) for n in range(2)]
        ohs = sb("ohs", [P, NE])
        seen = sb("seen", [P, NE], bf16)
        rk = sb("rk", [P, NJ, NE])
        rank = sb("rank", [P, NJ])
        sl_a = sb("sl_a", [P, NJ])
        sl_o = sb("sl_o", [P, NJ])
        slot = sb("slot", [P, NB, NJ], i32)

        w1 = [sb(f"w1_{n}", [P, 2, FF]) for n in range(2)]
        w2 = [sb(f"w2_{n}", [P, 2, NF, D]) for n in range(2)]
        hin = [sb(f"hin{n}", [P, NS, D]) for n in range(2)]
        rest = [sb(f"rest{n}", [P, NS, ROW - D]) for n in range(2)]
        HT = [sb(f"HT{n}", [P, NF, CAP]) for n in range(2)]
        OT = qkn[:, 0:NS, :].rearrange("p n d -> p (n d)")
        yw = junk[:, 0:NS, :]
        x_tiles = x_all[:, :, :, :].rearrange("p b j d -> p (b j) d")
        fin = [x_tiles[:, n * NS:(n + 1) * NS, :] for n in range(2)]
        with nc.sbuf_tensor("rows", [P, NB, NJ, ROW], f32) as rows:
            pass
        w1h, w1l, xth, xtl = [
            [sb(f"{name}{n}", shape, f32r) for n in range(2)]
            for name, shape in (("w1h", [P, 2, NF, P]), ("w1l", [P, 2, NF, P]),
                                ("xth", [P, PS]), ("xtl", [P, PS]))]

        x_in = [sem(f"x_in{n}") for n in range(NB)]
        c_in, wmod_in, w_in, blank_out = [sem(n) for n in ("c_in", "wmod_in", "w_in", "blank_out")]
        mod1_done = sem("mod1_done")
        consts, c_step, mod_ps, mod_step, mod_done = [
            sem(n) for n in ("consts", "c_step", "mod_ps", "mod_step", "mod_done")]
        pool_setup = sem("pool_setup")
        wt_ps, wt_done, diag_done, row_ps, row_done = [
            sem(n) for n in ("wt_ps", "wt_done", "diag_done", "row_ps", "row_done")]
        (ln1_st, ln1_mv, ln1_ln, ln1_rs, xh_done, xhT_ps, hT_done, hsq_done, mh_ps,
         qk_ps, v_ps, ssq_done, nrm_a, nrm_b, nrl_done, nrr_done, qkn_done,
         ew_done, kv_done, pair_done) = [sem(n) for n in (
             "ln1_st", "ln1_mv", "ln1_ln", "ln1_rs", "xh_done", "xhT_ps", "hT_done", "hsq_done",
             "mh_ps", "qk_ps", "v_ps", "ssq_done", "nrm_a",
             "nrm_b", "nrl_done", "nrr_done", "qkn_done", "ew_done", "kv_done", "pair_done")]
        (eqT_ps, sumw_ps, sumkv_ps, lq_done, lw_done, lden_done, rden_done, yT_done, u_ps, g_ps,
         gc_done, eg_done, lg_done, sg_done, gs_done, GT_done) = [sem(n) for n in (
             "eqT_ps", "sumw_ps", "sumkv_ps", "lq_done", "lw_done", "lden_done", "rden_done",
             "yT_done", "u_ps", "g_ps", "gc_done", "eg_done", "lg_done", "sg_done", "gs_done",
             "GT_done")]
        (x1_ps, x1_done, ln2_st, ln2_mv, ln2_ln, ln2_rs, nm2_done, xh2_done, xh2T_ps, h2T_done, h2_ps,
         h2_done, logit_ps, mx_done, dl_done, pe_done, psm_done, prob_done, cand_done, best_done,
         oh_done, ohs_done, seen_done, rank_ps, rk_done, rank_done, sl_done, slot_done,
         gp_done) = [sem(n) for n in (
             "x1_ps", "x1_done", "ln2_st", "ln2_mv", "ln2_ln", "ln2_rs", "nm2_done", "xh2_done", "xh2T_ps",
             "h2T_done", "h2_ps", "h2_done", "logit_ps", "mx_done", "dl_done", "pe_done",
             "psm_done", "prob_done", "cand_done", "best_done", "oh_done", "ohs_done",
             "seen_done", "rank_ps", "rk_done", "rank_done", "sl_done", "slot_done", "gp_done")]
        pool_past = sem("pool_past")
        w1h_done, w1l_done, xth_done = sem("w1h_done"), sem("w1l_done"), sem("xth_done")
        x1_out, scattered = sem("x1_out"), sem("scattered")
        w1_in = [sem(f"w1_in{n}") for n in range(2)]
        w2_in = [sem(f"w2_in{n}") for n in range(2)]
        hin_in = [sem(f"hin_in{n}") for n in range(2)]
        rest_in = [sem(f"rest_in{n}") for n in range(2)]
        final_out = [sem(f"final_out{n}") for n in range(2)]
        xt_ps, xt_done, h_ps, h_done, o_ps, o_done, y_ps, yw_done, fin_done = [
            sem(n) for n in ("xt_ps", "xt_done", "h_ps", "h_done", "o_ps", "o_done", "y_ps",
                             "yw_done", "fin_done")]

        def after(eng, s, b, lag=0):
            if isinstance(b, int) and b - lag < 0:
                return
            eng.wait_ge(s, b + 1 - lag)

        def carry_waits(eng, s):
            eng.sem_inc(s, 1)

        def batches(steps, early=(), first=None, second=None):
            for i in range(NB + max(lag for lag, _ in steps)):
                for lag, step in steps:
                    if 0 <= i - lag < NB and not (i == lag and step in early):
                        step(i - lag)
                if i == 0 and first:
                    first()
                if i == 1 and second:
                    second()

        freed = {"v": (mod_step, 2), "w": (mod1_done, 1)}

        def claim(pe, bank, reader, b):
            if bank in freed:
                pe.wait_ge(*freed[bank])
            freed[bank] = (reader, b + 1)

        HEAD = CAP // P
        LAST_PARTS = ((NPAIR - 1, 0, HEAD), (NPAIR, HEAD, NS))

        def in_pairs(eng, chain):
            for i in range(2):
                chain(i, i % 2, i // 2)
            with eng.Fori(1, NPAIR // 2 - 1) as p:
                for u in range(2):
                    chain(2 * p + u, u, p)
            for i in range(NPAIR - 2, NPAIR):
                chain(i, i % 2, i // 2)

        block = ctx.enter_context(nc.Block())

        @block.sync
        def _(sp):
            sp.dma_start(c_sb[:, :], c_d).then_inc(c_in, 16)
            x_v = x_d.rearrange("b (j p) d -> p b j d", p=P)
            sp.dma_start(x_all[:, 0, :, :], x_v[:, 0, :, :]).then_inc(x_in[0], 16)
            sp.dma_start(wmod[:, :, :], wmod_d.rearrange("i (m d) -> i m d", m=6)
                         ).then_inc(wmod_in, 16)
            sp.dma_start(wqkv[:, :, :], w_qkv_d.rearrange("(m e) d -> e m d", m=3)).then_inc(w_in, 16)
            sp.dma_start(wsw[:, :, :], w_swiglu_d.rearrange("(m e) d -> e m d", m=2)).then_inc(w_in, 16)
            sp.dma_start(wout[:, :], w_out_d).then_inc(w_in, 16)
            sp.dma_start(gw[:, :], gate_w_d).then_inc(w_in, 16)
            for b in range(1, NB):
                sp.dma_start(x_all[:, b, :, :], x_v[:, b, :, :]).then_inc(x_in[b], 16)
            sp.wait_ge(pool_setup, 8)
            disp_v = disp_d.rearrange("(n p) c -> p n c", p=P)
            for q in range(NPAIR):
                sp.dma_start(disp_v[:, q * NS:(q + 1) * NS, :],
                             blank[:, :].unsqueeze(1).to_broadcast([P, NS, ROW])).then_inc(blank_out, 16)

            def load_w1(i, par):
                sp.dma_start(w1[par][:, :, :], w1_d[bass.ds(2 * i, 2), :, :].rearrange("e d f -> d e f")
                             ).then_inc(w1_in[par], 16)

            def load_w2(i, par):
                sp.dma_start(w2[par][:, :, :, :].rearrange("p e f d -> p e (f d)"),
                             w2_d[bass.ds(2 * i, 2), :, :].rearrange("e (p f) d -> p e (f d)", f=NF)
                             ).then_inc(w2_in[par], 16)

            for i in range(2):
                load_w1(i, i)
                load_w2(i, i)
            for b in range(NB):
                sp.wait_ge(x1_done, b + 1)
                sp.dma_start(out_d[b, :, :].rearrange("(j p) d -> p j d", p=P),
                             rows[:, b, :, C_X1:C_X1 + D]).then_inc(x1_out, 16)
            sp.wait_ge(scattered, 16 * NB * NJ)

            def slots_of(i):
                return disp_d[bass.ds(i * PS, PS), :].rearrange("(n p) c -> p n c", p=P)

            def load_h2(i, par):
                sp.dma_start(hin[par][:, :, :], slots_of(i)[:, :, 0:D]).then_inc(hin_in[par], 16)

            def load_pair(i, par, k):
                if not isinstance(i, int) or 1 <= i < NPAIR - 1:
                    sp.wait_ge(xt_ps, i)
                if not (isinstance(i, int) and i == NPAIR - 1):
                    load_h2(i + 1, 1 - par)
                if not isinstance(i, int) or 1 <= i < NPAIR - 1:
                    sp.wait_ge(w1l_done, i)
                    load_w1(i + 1, 1 - par)
                if not isinstance(i, int) or i >= 2:
                    sp.wait_ge(o_ps, 2 * i - 2)
                    load_w2(i, par)
                    sp.wait_ge(final_out[par], 16 * NS * k)
                sp.dma_start(rest[par][:, :, :], slots_of(i)[:, :, D:ROW]).then_inc(rest_in[par], 16)

            load_h2(0, 0)
            in_pairs(sp, load_pair)
            sp.wait_ge(x1_out, 16 * NB)
            for par in range(2):
                sp.wait_ge(final_out[par], 16 * NS * NPAIR // 2)

        @block.gpsimd
        def _(pool):
            pool.memset(ident[:, :], 0.0).then_inc(pool_setup, 1)
            pool.memset(tri[:, :], 1.0).then_inc(pool_setup, 1)
            pool.memset(blank[:, :], 0.0).then_inc(pool_setup, 1)
            pool.memset(ones_b[:, :], 1.0).then_inc(pool_setup, 1)
            pool.memset(seen[:, :], 0.0).then_inc(pool_setup, 1)
            pool.iota(rev_i[:, :], pattern=[[0, NJ], [-1, NE]], base=NE, channel_multiplier=0
                      ).then_inc(pool_setup, 1)
            pool.iota(tokid[:, :], pattern=[[P, NTOK // P]], base=0, channel_multiplier=1
                      ).then_inc(pool_setup, 1)
            pool.wait_ge(pool_setup, 7)
            pool.memset(blank[:, C_TOK:C_TOK + 1].bitcast(i32), NOWHERE).then_inc(pool_setup, 1)
            pool.affine_select(out=ident[:, :], in_=ident[:, :], compare_op=ALU.not_equal, fill=1.0,
                               base=0, pattern=[[-1, P]], channel_multiplier=1).then_inc(consts, 1)
            pool.affine_select(out=tri[:, 0:P], in_=tri[:, 0:P], compare_op=ALU.is_ge, fill=0.0,
                               base=0, pattern=[[1, P]], channel_multiplier=-1).then_inc(consts, 1)
            pool.wait_ge(consts, 2)
            pool.tensor_copy(tri_b[:, :], tri[:, 0:P]).then_inc(consts, 1)
            rows_t = rows[:, :, :, :].rearrange("p b j c -> p (b j) c")
            pool.tensor_copy(rows_t[:, :, C_TOK].bitcast(i32), tokid[:, :])
            pool.memset(rows_t[:, :, C_TOK + 1], 0.0)
            pool.tensor_copy(rev[:, :, :].rearrange("p j e -> p (j e)"), rev_i[:, :]).then_inc(consts, 1)

            def squares(b):
                after(pool, hT_done, b)
                after(pool, mh_ps, b, 1)
                pool.tensor_tensor(hsq[:, :], hT[b % NHT][:, :], hT[b % NHT][:, :], ALU.mult
                                   ).then_inc(hsq_done, 1)

            def pair_sums(b):
                after(pool, kv_done, b)
                t = ewkv[b % 2]
                pool.tensor_tensor(t[:, NJ, 1:3, :], t[:, 0, 1:3, :], t[:, 1, 1:3, :], ALU.add
                                   ).then_inc(pair_done, 1)

            def log_denominator(b):
                after(pool, lq_done, b)
                after(pool, lw_done, b)
                after(pool, rden_done, b, 1)
                pool.tensor_tensor(lden[:, :], lq[:, :], lw[:, :], ALU.add).then_inc(lden_done, 1)

            def silu(b):
                after(pool, gc_done, b)
                after(pool, sg_done, b)
                after(pool, GT_done, b, 1)
                pool.tensor_tensor(gs[:, :], gc[:, :], sg[:, :], ALU.mult).then_inc(gs_done, 1)

            def gate_rows(b):
                if b == 0:
                    pool.wait_ge(row_done, 4)
                after(pool, prob_done, b)
                pool.tensor_tensor(rows[:, b, :, C_GP:C_GP + D],
                                   gb_row[:, b, :].unsqueeze(1).to_broadcast([P, NJ, D]),
                                   prob[:, :].unsqueeze(2).to_broadcast([P, NJ, D]), ALU.mult
                                   ).then_inc(gp_done, 1)

            def scatter(b):
                if b == 0:
                    pool.wait_ge(blank_out, 16 * NPAIR)
                pool.wait_ge(gp_done, b + 1)
                after(pool, h2_done, b)
                after(pool, slot_done, b)
                for j in range(NJ):
                    pool.indirect_dma_start(
                        out=disp_d, out_offset=bass.IndirectOffsetOnAxis(ap=slot[:, b, j:j + 1], axis=0),
                        in_=rows[:, b, j, :], in_offset=None, bounds_check=NSLOT - 1,
                        oob_is_err=False).then_inc(scattered, 16)

            batches([
                (3, silu), (2, log_denominator), (0, squares), (5, gate_rows),
                (1, pair_sums), (5, scatter)])

            pool.wait_ge(x1_out, 16 * NB)

            last_token = pool.to_reg(NTOK - 1)

            def send(i, par, k):
                if isinstance(i, int) and i == NPAIR - 1:
                    for part, n0, n1 in LAST_PARTS:
                        send_tiles(part, par, n0, n1)
                else:
                    send_tiles(i, par, 0, NS)

            def send_tiles(i, par, n0, n1):
                after(pool, fin_done, i)
                carry_waits(pool, pool_past)
                for n in range(n0, n1):
                    pool.indirect_dma_start(
                        out=out_d.rearrange("b t d -> (b t) d"),
                        out_offset=bass.IndirectOffsetOnAxis(
                            ap=rest[par][:, n, C_TOK - D:C_TOK - D + 1].bitcast(i32), axis=0),
                        in_=fin[par][:, n, :], in_offset=None, bounds_check=last_token,
                        oob_is_err=False).then_inc(final_out[par], 16)

            in_pairs(pool, send)

        @block.scalar
        def _(act):
            act.preload_act_table_set("natural_log_exp_and_others")
            def ln1_scale(b):
                after(act, ln1_mv, b)
                act.activation(ln1[:, :], mv1[:, :, 1], ACT.Ln, bias=eps[:, 0:1]).then_inc(ln1_ln, 1)
                act.wait_ge(ln1_ln, b + 1)
                after(act, xh_done, b, 1)
                act.activation(rs1[:, :], ln1[:, :], ACT.Exp, scale=-0.5).then_inc(ln1_rs, 1)

            def modulate1(b):
                after(act, xhT_ps, b)
                after(act, x1_ps, b, NHT)
                if b == 0:
                    act.wait_ge(mod1_done, 1)
                act.activation(hT[b % NHT][:, :], ps_t, ACT.Identity, bias=mod[:, SA, b:b + 1],
                               scale=mod[:, CA, b:b + 1]).then_inc(hT_done, 1)

            def square_sums(b):
                after(act, qk_ps, b)
                after(act, nrm_b, b, 1)
                for j in range(NJ):
                    for m in range(2):
                        last = act.activation(junk[:, 2 * j + m, :], ps_qk[:, j, m * D:(m + 1) * D],
                                              ACT.Square, accum_out=ssq[:, j, m:m + 1])
                last.then_inc(ssq_done, 1)

            def rms_scales(b):
                after(act, nrm_b, b)
                act.activation(nrl[:, :], nrm[:, :], ACT.Ln).then_inc(nrl_done, 1)
                act.wait_ge(nrl_done, b + 1)
                after(act, kv_done, b, 1)
                act.activation(nrr[:, :], nrl[:, :], ACT.Exp, scale=-0.5).then_inc(nrr_done, 1)

            def exp_qk(b):
                after(act, qkn_done, b)
                after(act, sumkv_ps, b, 2)
                after(act, eqT_ps, b, 2)
                act.activation(ewkv[b % 2][:, 0:NJ, 0:2, :].rearrange("p j m d -> p j (m d)"),
                               qkn[:, :, :].rearrange("p (j m) d -> p j (m d)", m=2),
                               ACT.Exp).then_inc(ew_done, 1)

            def log_q(b):
                after(act, eqT_ps, b)
                after(act, lden_done, b, 1)
                act.activation(lq[:, :], ps_g, ACT.Ln, bias=eps[:, 2:3]).then_inc(lq_done, 1)

            def log_w(b):
                after(act, sumw_ps, b)
                after(act, lden_done, b, 1)
                act.activation(lw[:, :], ps_w, ACT.Ln, bias=eps[:, 1:2]).then_inc(lw_done, 1)

            def reciprocal(b):
                after(act, lden_done, b)
                after(act, yT_done, b, 1)
                act.activation(rden[:, :], lden[:, :], ACT.Exp, scale=-1.0).then_inc(rden_done, 1)

            def exp_g(b):
                after(act, gc_done, b)
                act.activation(eg[:, :], gc[:, :], ACT.Exp, scale=-1.0).then_inc(eg_done, 1)

            def log_g(b):
                act.wait_ge(eg_done, b + 1)
                act.activation(lg[:, :], eg[:, :], ACT.Ln, bias=eps[:, 2:3]).then_inc(lg_done, 1)

            def sigmoid_g(b):
                act.wait_ge(lg_done, b + 1)
                after(act, gs_done, b, 1)
                act.activation(sg[:, :], lg[:, :], ACT.Exp, scale=-1.0).then_inc(sg_done, 1)

            def ln2_scale(b):
                after(act, ln2_mv, b)
                act.activation(ln2[:, :], mv2[:, :, 1], ACT.Ln, bias=eps[:, 0:1]).then_inc(ln2_ln, 1)
                act.wait_ge(ln2_ln, b + 1)
                act.activation(rs2[:, :], ln2[:, :], ACT.Exp, scale=-0.5).then_inc(ln2_rs, 1)

            def normalize2(b):
                after(act, nm2_done, b)
                after(act, xh2T_ps, b, 1)
                for j in range(NJ):
                    last = act.activation(xh2[:, j, :], rows[:, b, j, C_X1:C_X1 + D], ACT.Identity,
                                          bias=nm2[:, j:j + 1], scale=rs2[:, j:j + 1])
                last.then_inc(xh2_done, 1)

            def modulate2(b):
                if b == 0:
                    act.wait_ge(mod_done, 1)
                after(act, xh2T_ps, b)
                after(act, h2_ps, b, 1)
                act.activation(h2T[:, :], ps_t, ACT.Identity, bias=mod[:, SB, b:b + 1],
                               scale=mod[:, CB, b:b + 1]).then_inc(h2T_done, 1)

            def h2_rows(b):
                after(act, h2_ps, b)
                act.copy(rows[:, b, :, 0:D], ps_g.rearrange("p (j d) -> p j d", d=D)).then_inc(h2_done, 1)

            def exp_logits(b):
                after(act, dl_done, b)
                after(act, psm_done, b, 1)
                act.activation(pe_[:, :, :], dl[:, :, :], ACT.Exp).then_inc(pe_done, 1)

            act.wait_ge(c_in, 16)
            act.activation(c_e[:, :], c_sb[:, :], ACT.Exp, scale=-1.0).then_inc(c_step, 1)
            ln1_scale(0)
            act.wait_ge(wt_ps, 1)
            act.mul(wqkvT[:, 0:D], bank01[:, 0:D], -1.0)
            act.copy(wqkvT[:, D:3 * D], bank01[:, D:3 * D])
            act.copy(wswT[:, :], bank01[:, 512:512 + 2 * D])
            act.copy(gwT[:, :], bank01[:, 512 + 2 * D:512 + 2 * D + NE]).then_inc(wt_done, 1)

            def copy_rows():
                for n, (dst, src) in enumerate(((woga, ps_w), (woga, ps_kv), (gb_row, ps_u), (gb_row, ps_t))):
                    act.wait_ge(row_ps, n + 1)
                    half = n % 2
                    act.copy(dst[:, 4 * half:4 * half + 4, :], src.rearrange("p (b d) -> p b d", d=D)
                             ).then_inc(row_done, 1)

            batches([
                (5, normalize2), (3, reciprocal), (0, ln1_scale), (2, log_q),
                (1, square_sums), (5, modulate2), (3, exp_g), (1, rms_scales), (3, log_g),
                (2, log_w), (3, sigmoid_g), (0, modulate1), (4, ln2_scale), (5, h2_rows),
                (5, exp_logits), (1, exp_qk)], early=(ln1_scale,), second=copy_rows)

            HB = 3

            def w1_high(i, par, k):
                act.wait_ge(w1_in[par], 16 * (k + 1))
                if not isinstance(i, int) or i >= 2:
                    act.wait_ge(h_ps, 2 * NF * (i - 1))
                act.copy(w1h[par][:, :, :, :], w1[par][:, :, :].rearrange("p e (m f) -> p e f m", f=NF)
                         ).then_inc(w1h_done, 1)

            def xt_high(i, par):
                after(act, xt_ps, i)
                if not isinstance(i, int) or i >= 2:
                    act.wait_ge(h_ps, 2 * NF * (i - 1))
                act.copy(xth[par][:, :], ps_xt).then_inc(xth_done, 1)

            act.preload_act_table_set("gelu_apprx_tanh_and_others")
            act.wait_ge(scattered, 16 * NB * NJ)
            act.wait_ge(x1_out, 16 * NB)
            w1_high(0, 0, 0)
            xt_high(0, 0)

            def experts(i, par, k):
                last = isinstance(i, int) and i == NPAIR - 1
                for c in range(2 * NF):
                    e, f = c // NF, c % NF
                    if c == 2 * NF - 1 and not last:
                        w1_high(i + 1, 1 - par, k + par)
                        xt_high(i + 1, 1 - par)
                    act.wait_ge(h_ps, 2 * NF * i + c + 1)
                    if f == 0 and (not isinstance(i, int) or i >= 1):
                        act.wait_ge(o_ps, 2 * i - 1 + e)
                    act.activation(HT[e][:, f, :], ps_h[c % HB][:, 0:CAP], ACT.Gelu_apprx_tanh
                                   ).then_inc(h_done, 1)

            in_pairs(act, experts)

        @block.vector
        def _(dve):
            def stats1(b):
                dve.wait_ge(x_in[b], 16)
                for j in range(NJ):
                    last = dve.bn_stats(st1[:, j, :], x_all[:, b, j, :])
                last.then_inc(ln1_st, 1)

            def aggregate1(b):
                dve.wait_ge(ln1_st, b + 1)
                after(dve, ln1_ln, b, 1)
                for j in range(NJ):
                    last = dve.bn_aggr(mv1[:, j, :], st1[:, j, :])
                last.then_inc(ln1_mv, 1)

            def normalize1(b):
                after(dve, ln1_rs, b)
                after(dve, xhT_ps, b, 1)
                for j in range(NJ):
                    last = dve.tensor_scalar(xh[:, j, :], x_all[:, b, j, :], mv1[:, j, 0:1],
                                             rs1[:, j:j + 1], ALU.subtract, ALU.mult)
                last.then_inc(xh_done, 1)

            def h_means(b):
                after(dve, mh_ps, b)
                after(dve, nrl_done, b, 1)
                dve.tensor_scalar(nrm[:, 2 * NJ:3 * NJ], ps_mh, 1.0 / D, EPS_RMS, ALU.mult, ALU.add)
                dve.tensor_scalar(mh[:, :], ps_mh, EPS_RMS / D, EPS_RMS * EPS_RMS, ALU.mult, ALU.add
                                  ).then_inc(nrm_a, 1)

            def qk_means(b):
                after(dve, ssq_done, b)
                dve.wait_ge(nrm_a, b + 1)
                dve.scalar_tensor_tensor(nrm[:, 0:2 * NJ].rearrange("p (j m) -> p j m", m=2), ssq[:, :, :],
                                         1.0 / D, mh[:, :].unsqueeze(2).to_broadcast([P, NJ, 2]),
                                         ALU.mult, ALU.add).then_inc(nrm_b, 1)

            def normalize_qk(b):
                after(dve, nrr_done, b)
                after(dve, qk_ps, b)
                after(dve, ssq_done, b)
                after(dve, ew_done, b, 1)
                dve.tensor_tensor(qkn[:, :, :], ps_qk.rearrange("p j (m d) -> p (j m) d", m=2),
                                  nrr[:, 0:2 * NJ].unsqueeze(2).to_broadcast([P, 2 * NJ, D]), ALU.mult
                                  ).then_inc(qkn_done, 1)

            def weigh_v(b):
                after(dve, v_ps, b)
                after(dve, ew_done, b)
                t = ewkv[b % 2]
                for j in range(NJ):
                    last = dve.scalar_tensor_tensor(t[:, j, 2, :], ps_v[:, j, :],
                                                    nrr[:, 2 * NJ + j:2 * NJ + j + 1],
                                                    t[:, j, 1, :], ALU.mult, ALU.mult)
                last.then_inc(kv_done, 1)

            def divide(b):
                after(dve, rden_done, b)
                after(dve, sumkv_ps, b)
                after(dve, u_ps, b, 1)
                dve.tensor_tensor(yT[:, :], ps_kv, rden[:, :], ALU.mult).then_inc(yT_done, 1)

            def clamp_g(b):
                after(dve, g_ps, b)
                after(dve, gs_done, b, 1)
                dve.tensor_scalar(gc[:, :], ps_g, -43.0, None, ALU.max).then_inc(gc_done, 1)

            def gate_u(b):
                after(dve, gs_done, b)
                after(dve, u_ps, b)
                after(dve, x1_ps, b, 2)
                dve.tensor_tensor(GT[b % 2][:, :], gs[:, :], ps_u, ALU.mult).then_inc(GT_done, 1)

            def residual(b):
                after(dve, x1_ps, b)
                dve.tensor_tensor(rows[:, b, :, C_X1:C_X1 + D], x_all[:, b, :, :],
                                  ps_u.rearrange("p (j d) -> p j d", d=D), ALU.add).then_inc(x1_done, 1)

            def stats2(b):
                dve.wait_ge(x1_done, b + 1)
                for j in range(NJ):
                    last = dve.bn_stats(st2[:, j, :], rows[:, b, j, C_X1:C_X1 + D])
                last.then_inc(ln2_st, 1)

            def aggregate2(b):
                dve.wait_ge(ln2_st, b + 1)
                after(dve, ln2_ln, b, 1)
                for j in range(NJ):
                    last = dve.bn_aggr(mv2[:, j, :], st2[:, j, :])
                last.then_inc(ln2_mv, 1)

            def shift2(b):
                after(dve, ln2_rs, b)
                after(dve, xh2_done, b, 1)
                dve.scalar_tensor_tensor(nm2[:, :], mv2[:, :, 0], -1.0, rs2[:, :], ALU.mult, ALU.mult
                                         ).then_inc(nm2_done, 1)

            def top1(b):
                after(dve, logit_ps, b)
                lg_v = ps_logit.rearrange("p (j e) -> p j e", e=NE)
                dve.tensor_reduce(mx[:, :], lg_v, X, ALU.max).then_inc(mx_done, 1)
                dve.wait_ge(mx_done, b + 1)
                after(dve, pe_done, b, 1)
                dve.tensor_tensor(dl[:, :, :], lg_v, mx[:, :].unsqueeze(2).to_broadcast([P, NJ, NE]),
                                  ALU.subtract).then_inc(dl_done, 1)
                dve.wait_ge(dl_done, b + 1)
                dve.scalar_tensor_tensor(cand[:, :, :], dl[:, :, :], 0.0, rev[:, :, :], ALU.is_ge, ALU.mult
                                         ).then_inc(cand_done, 1)
                dve.wait_ge(cand_done, b + 1)
                dve.tensor_reduce(best[:, b, :], cand[:, :, :], X, ALU.max).then_inc(best_done, 1)
                dve.wait_ge(best_done, b + 1)
                dve.tensor_tensor(oh[b % 2][:, :, :], rev[:, :, :],
                                  best[:, b, :].unsqueeze(2).to_broadcast([P, NJ, NE]),
                                  ALU.is_equal).then_inc(oh_done, 1)

            def top_prob(b):
                after(dve, pe_done, b)
                dve.tensor_reduce(psm[:, :], pe_[:, :, :], X, ALU.add).then_inc(psm_done, 1)
                dve.wait_ge(psm_done, b + 1)
                after(dve, gp_done, b, 1)
                dve.reciprocal(prob[:, :], psm[:, :]).then_inc(prob_done, 1)

            def slots(b):
                dve.wait_ge(oh_done, b + 1)
                dve.tensor_reduce(ohs[:, :], oh[b % 2][:, :, :].rearrange("p j e -> p e j"), X, ALU.add
                                  ).then_inc(ohs_done, 1)
                after(dve, rank_ps, b)
                dve.tensor_tensor(rk[:, :, :], oh[b % 2][:, :, :],
                                  ps_rank.rearrange("p (j e) -> p j e", e=NE), ALU.mult
                                  ).then_inc(rk_done, 1)
                dve.wait_ge(ohs_done, b + 1)
                dve.tensor_tensor(seen[:, :], seen[:, :], ohs[:, :], ALU.add).then_inc(seen_done, 1)
                dve.wait_ge(rk_done, b + 1)
                dve.tensor_reduce(rank[:, :], rk[:, :, :], X, ALU.add).then_inc(rank_done, 1)
                dve.wait_ge(rank_done, b + 1)
                dve.scalar_tensor_tensor(sl_a[:, :], best[:, b, :], -float(CAP), rank[:, :], ALU.mult, ALU.add)
                dve.tensor_scalar(sl_o[:, :], rank[:, :], float(CAP), float(NOWHERE), ALU.is_gt, ALU.mult
                                  ).then_inc(sl_done, 1)
                dve.wait_ge(sl_done, b + 1)
                dve.scalar_tensor_tensor(slot[:, b, :], sl_a[:, :], float(NE * CAP - 1), sl_o[:, :],
                                         ALU.add, ALU.add).then_inc(slot_done, 1)

            dve.memset(eps[:, 0:1], EPS_LN)
            dve.memset(eps[:, 1:2], 1e-06)
            dve.memset(eps[:, 2:4], 1.0).then_inc(mod_step, 1)
            dve.wait_ge(c_step, 1)
            dve.tensor_scalar(c_e[:, :], c_e[:, :], 1.0, None, ALU.add).then_inc(c_step, 1)
            dve.wait_ge(c_step, 2)
            dve.reciprocal(c_e[:, :], c_e[:, :]).then_inc(c_step, 1)
            dve.wait_ge(c_step, 3)
            dve.tensor_tensor(c_s[:, :], c_sb[:, :], c_e[:, :], ALU.mult).then_inc(c_step, 1)
            dve.wait_ge(mod_ps, 1)
            dve.tensor_copy(c_T[:, :], bank3[:, 0:NB]).then_inc(c_step, 1)
            stats1(0)
            aggregate1(0)
            dve.wait_ge(mod_ps, 2)
            dve.tensor_copy(mod[:, SA, :], bank4[:, SA * NB:(SA + 1) * NB])
            dve.tensor_scalar(mod[:, CA, :], bank4[:, CA * NB:(CA + 1) * NB], 1.0, None, ALU.add
                              ).then_inc(mod1_done, 1)
            normalize1(0)
            dve.wait_ge(mod_ps, 3)
            dve.tensor_copy(mod_r[:, GA:, :], bank3[:, 64 + GA * NB:64 + 6 * NB].rearrange(
                "p (m b) -> p m b", b=NB)).then_inc(mod_step, 1)
            dve.wait_ge(mod_step, 2)
            for n, m in enumerate((GA, GB)):
                dve.tensor_scalar(sgn[:, n, :], mod_r[:, m, :], 0.0, 2.0, ALU.is_ge, ALU.mult)
                dve.tensor_scalar(mod[:, m, :], mod_r[:, m, :], -1.0, None, ALU.mult)
            dve.tensor_scalar(mod[:, CB, :], mod_r[:, CB, :], 1.0, None, ALU.add)
            dve.tensor_copy(mod[:, SB, :], mod_r[:, SB, :]).then_inc(mod_step, 1)
            dve.wait_ge(mod_step, 3)
            for m in (GA, GB):
                last = dve.tensor_tensor(mod[:, m, :], mod[:, m, :], mod_r[:, m, :], ALU.max)
            last.then_inc(mod_step, 1)
            dve.wait_ge(mod_step, 4)
            for m in (GA, GB):
                last = dve.tensor_scalar(mod[:, m, :], mod[:, m, :], 0.25, None, ALU.max)
            last.then_inc(mod_step, 1)
            dve.wait_ge(mod_step, 5)
            for n, m in enumerate((GA, GB)):
                last = dve.scalar_tensor_tensor(mod[:, m, :], sgn[:, n, :], -1.0, mod[:, m, :],
                                                ALU.add, ALU.mult)
            last.then_inc(mod_done, 1)

            def diagonals():
                dve.wait_ge(mod_done, 1)
                for dst, m in ((diag_ga, GA), (diag_gb, GB)):
                    dve.tensor_tensor(dst[:, :, :], ident[:, :].unsqueeze(1).to_broadcast([P, NB, D]),
                                      mod[:, m, :].unsqueeze(2).to_broadcast([P, NB, D]), ALU.mult
                                      ).then_inc(diag_done, 1)

            dve.wait_ge(consts, 4)
            batches([
                (0, stats1), (0, aggregate1), (2, weigh_v), (3, divide), (0, normalize1),
                (1, h_means), (3, clamp_g), (4, residual), (1, qk_means), (4, stats2),
                (1, normalize_qk), (4, aggregate2), (5, top1), (4, shift2), (3, gate_u),
                (5, top_prob), (5, slots)], early=(stats1, aggregate1, normalize1), second=diagonals)

            def w1_low(i, par):
                after(dve, w1h_done, i)
                dve.tensor_tensor(w1l[par][:, :, :, :],
                                  w1[par][:, :, :].rearrange("p e (m f) -> p e f m", f=NF),
                                  w1h[par][:, :, :, :].bitcast(f32), ALU.subtract).then_inc(w1l_done, 1)

            def xt_low(i, par):
                after(dve, xth_done, i)
                dve.tensor_tensor(xtl[par][:, :], ps_xt, xth[par][:, :].bitcast(f32), ALU.subtract
                                  ).then_inc(xt_done, 1)

            def combine(i, par, k, n0=0, n1=NS):
                after(dve, y_ps, i)
                dve.wait_ge(rest_in[par], 16 * (k + 1))
                after(dve, fin_done, i, 1)
                dve.tensor_tensor(yw[:, n0:n1, :], ps_y.rearrange("p (n d) -> p n d", d=D)[:, n0:n1, :],
                                  rest[par][:, n0:n1, C_GP - D:C_GP], ALU.mult).then_inc(yw_done, 1)
                dve.wait_ge(yw_done, i + 1)
                if not isinstance(i, int) or i >= 2:
                    dve.wait_ge(final_out[par], 16 * NS * k)
                dve.tensor_tensor(fin[par][:, n0:n1, :], yw[:, n0:n1, :],
                                  rest[par][:, n0:n1, C_X1 - D:C_X1], ALU.add).then_inc(fin_done, 1)

            def experts(i, par, k):
                if not isinstance(i, int) or i >= 1:
                    combine(i - 1, 1 - par, k - 1 + par)
                if not (isinstance(i, int) and i == NPAIR - 1):
                    w1_low(i + 1, 1 - par)
                for e in range(2):
                    dve.wait_ge(o_ps, 2 * i + e + 1)
                    if e == 0:
                        after(dve, y_ps, i, 1)
                    dve.tensor_copy(OT[:, e * CAP:(e + 1) * CAP], ps_o).then_inc(o_done, 1)
                    if e == 0 and not (isinstance(i, int) and i == NPAIR - 1):
                        xt_low(i + 1, 1 - par)
                    if isinstance(i, int) and i == NPAIR - 1:
                        part, n0, n1 = LAST_PARTS[e]
                        combine(part, par, k, n0, n1)

            w1_low(0, 0)
            xt_low(0, 0)
            in_pairs(dve, experts)

        @block.tensor
        def _(pe):
            def transpose1(b):
                after(pe, xh_done, b)
                claim(pe, "t", hT_done, b)
                for j in range(NJ):
                    last = pe.transpose(ps_t[:, j * P:(j + 1) * P], xh[:, j, :], ident[:, :])
                last.then_inc(xhT_ps, 1)

            def h_square_sums(b):
                after(pe, hsq_done, b)
                claim(pe, "v", nrm_a, b)
                for j in range(NJ):
                    last = pe.matmul(ps_mh[:, j:j + 1], hsq[:, j * P:(j + 1) * P], tri[:, P:P + 1],
                                     start=True, stop=True)
                last.then_inc(mh_ps, 1)

            def project_qk(b):
                after(pe, hT_done, b)
                claim(pe, "qk", qkn_done, b)
                for j in range(NJ):
                    last = pe.matmul(ps_qk[:, j, :], hT[b % NHT][:, j * P:(j + 1) * P], wqkvT[:, 0:2 * D],
                                     start=True, stop=True)
                last.then_inc(qk_ps, 1)

            def project_v(b):
                after(pe, hT_done, b)
                claim(pe, "v", kv_done, b)
                for j in range(NJ):
                    last = pe.matmul(ps_v[:, j, :], hT[b % NHT][:, j * P:(j + 1) * P],
                                     wqkvT[:, 2 * D:3 * D], start=True, stop=True)
                last.then_inc(v_ps, 1)

            def transpose_q(b):
                after(pe, ew_done, b)
                claim(pe, "g", lq_done, b)
                for j in range(NJ):
                    last = pe.transpose(ps_g[:, j * P:(j + 1) * P], ewkv[b % 2][:, j, 0, :], ident[:, :])
                last.then_inc(eqT_ps, 1)

            def running_sum(ps, t, m):
                pe.matmul(ps[:, 0:2 * P], t[:, 0, m, :], tri[:, 0:2 * P], start=True, stop=False)
                pe.matmul(ps[:, P:2 * P], t[:, 1, m, :], tri[:, 0:P], start=False, stop=False)
                pe.matmul(ps[:, 2 * P:4 * P], t[:, NJ, m, :], tri[:, P:3 * P], start=False, stop=False)
                pe.matmul(ps[:, 2 * P:4 * P], t[:, 2, m, :], tri[:, 0:2 * P], start=False, stop=False)
                return pe.matmul(ps[:, 3 * P:4 * P], t[:, 3, m, :], tri[:, 0:P], start=False, stop=True)

            def sum_w(b):
                after(pe, pair_done, b)
                claim(pe, "w", lw_done, b)
                running_sum(ps_w, ewkv[b % 2], 1).then_inc(sumw_ps, 1)

            def sum_kv(b):
                after(pe, pair_done, b)
                claim(pe, "kv", yT_done, b)
                running_sum(ps_kv, ewkv[b % 2], 2).then_inc(sumkv_ps, 1)

            def project_g(b):
                after(pe, yT_done, b)
                claim(pe, "g", gc_done, b)
                pe.matmul(ps_g, wswT[:, D:2 * D], yT[:, :], start=True, stop=True).then_inc(g_ps, 1)

            def project_u(b):
                after(pe, yT_done, b)
                claim(pe, "u", GT_done, b)
                pe.matmul(ps_u, wswT[:, 0:D], yT[:, :], start=True, stop=True).then_inc(u_ps, 1)

            def project_out(b):
                after(pe, GT_done, b)
                claim(pe, "u", x1_done, b)
                for j in range(NJ):
                    pe.matmul(ps_u[:, j * P:(j + 1) * P], hT[b % NHT][:, j * P:(j + 1) * P],
                              diag_ga[:, b, :], start=True, stop=False)
                    last = pe.matmul(ps_u[:, j * P:(j + 1) * P], GT[b % 2][:, j * P:(j + 1) * P],
                                     woga[:, b, :], start=False, stop=True)
                last.then_inc(x1_ps, 1)

            def transpose2(b):
                after(pe, xh2_done, b)
                claim(pe, "t", h2T_done, b)
                for j in range(NJ):
                    last = pe.transpose(ps_t[:, j * P:(j + 1) * P], xh2[:, j, :], ident[:, :])
                last.then_inc(xh2T_ps, 1)

            def logits(b):
                after(pe, h2T_done, b)
                claim(pe, "w", dl_done, b)
                for j in range(NJ):
                    last = pe.matmul(ps_logit[:, j * NE:(j + 1) * NE], h2T[:, j * P:(j + 1) * P], gwT[:, :],
                                     start=True, stop=True)
                last.then_inc(logit_ps, 1)

            def h2_back(b):
                after(pe, h2T_done, b)
                claim(pe, "g", h2_done, b)
                for j in range(NJ):
                    last = pe.transpose(ps_g[:, j * P:(j + 1) * P], h2T[:, j * P:(j + 1) * P], ident[:, :])
                last.then_inc(h2_ps, 1)

            def ranks(b):
                after(pe, oh_done, b)
                after(pe, seen_done, b, 1)
                claim(pe, "t", rk_done, b)
                hot = oh[b % 2]
                pe.matmul(ps_rank, ones_b[:, :], seen[:, :].unsqueeze(1).to_broadcast([P, NJ, NE]),
                          start=True, stop=False)
                pe.matmul(ps_rank, tri_b[:, :], hot[:, :, :].rearrange("p j e -> p (j e)"),
                          start=False, stop=False)
                for j in range(NJ - 1):
                    last = pe.matmul(ps_rank[:, (j + 1) * NE:NJ * NE], ones_b[:, :],
                                     hot[:, j, :].unsqueeze(1).to_broadcast([P, NJ - 1 - j, NE]),
                                     start=False, stop=(j == NJ - 2))
                last.then_inc(rank_ps, 1)

            pe.wait_ge(consts, 4)
            pe.wait_ge(c_step, 4)
            pe.transpose(bank3[:, 0:NB], c_s[:, :], ident[0:NB, 0:NB]).then_inc(mod_ps, 1)
            pe.wait_ge(c_step, 5)
            pe.wait_ge(wmod_in, 16)
            for m in (SA, CA):
                last = pe.matmul(bank4[:, m * NB:(m + 1) * NB], wmod[:, m, :], c_T[:, :],
                                 start=True, stop=True)
            last.then_inc(mod_ps, 1)
            pe.wait_ge(w_in, 64)
            for m in range(3):
                pe.transpose(bank01[:, m * D:(m + 1) * D], wqkv[:, m, :], ident[:, :])
            for m in range(2):
                pe.transpose(bank01[:, 512 + m * D:512 + (m + 1) * D], wsw[:, m, :], ident[:, :])
            pe.transpose(bank01[:, 512 + 2 * D:512 + 2 * D + NE], gw[:, :], ident[0:NE, 0:NE]
                         ).then_inc(wt_ps, 1)
            transpose1(0)
            for m in (GA, SB, CB, GB):
                last = pe.matmul(bank3[:, 64 + m * NB:64 + (m + 1) * NB], wmod[:, m, :], c_T[:, :],
                                 start=True, stop=True)
            last.then_inc(mod_ps, 1)
            pe.wait_ge(wt_done, 1)

            def row_products():
                pe.wait_ge(diag_done, 2)
                ones = tri[:, P:2 * P]
                for n, (bank, dst, lhsT, diag) in enumerate((
                        ("w", ps_w, wout[:, :], diag_ga), ("kv", ps_kv, wout[:, :], diag_ga),
                        ("u", ps_u, ones, diag_gb), ("t", ps_t, ones, diag_gb))):
                    claim(pe, bank, row_done, n)
                    half = n % 2
                    pe.matmul(dst, lhsT, diag[:, 4 * half:4 * half + 4, :].rearrange("p b d -> p (b d)"),
                              start=True, stop=True).then_inc(row_ps, 1)

            batches([
                (5, transpose2), (1, h_square_sums), (3, project_g), (2, sum_w),
                (0, transpose1), (2, sum_kv), (5, logits), (5, h2_back), (3, project_u),
                (1, project_v), (5, ranks), (0, project_qk), (1, transpose_q),
                (3, project_out)], early=(transpose1,), second=row_products)

            HB = 3

            def xt(i, par, k):
                pe.wait_ge(hin_in[par], 16 * (k + 1))
                after(pe, xt_done, i, 1)
                for n in range(NS):
                    last = pe.transpose(ps_xt[:, n * P:(n + 1) * P], hin[par][:, n, :], ident[:, :])
                last.then_inc(xt_ps, 1)

            def rows_back(i, outputs=None, n0=0, n1=NS):
                pe.wait_ge(o_done, 2 * i + 2 if outputs is None else outputs)
                after(pe, yw_done, i, 1)
                for n in range(n0, n1):
                    last = pe.transpose(ps_y[:, n * P:(n + 1) * P], OT[:, n * P:(n + 1) * P], ident[:, :])
                last.then_inc(y_ps, 1)

            def experts(i, par, k):
                first = isinstance(i, int) and i == 0
                after(pe, xt_done, i)
                after(pe, w1l_done, i)
                pe.wait_ge(w2_in[par], 16 * (k + 1))

                def inner(c):
                    e, f = c // NF, c % NF
                    if c >= HB:
                        pe.wait_ge(h_done, 2 * NF * i + c - HB + 1)
                    elif not first:
                        back = max(q for q in range(2 * NF) if q % HB == c)
                        pe.wait_ge(h_done, 2 * NF * i + (back - 2 * NF + 1))
                    for n, (w, x) in enumerate(((w1h, xth), (w1h, xtl), (w1l, xth))):
                        last = pe.matmul(ps_h[c % HB][:, 0:CAP], w[par][:, e, f, :],
                                         x[par][:, e * CAP:(e + 1) * CAP], start=(n == 0), stop=(n == 2))
                    last.then_inc(h_ps, 1)

                def outer(e):
                    if e == 1 or not first:
                        pe.wait_ge(o_done, 2 * i + e)
                    for f in range(NF):
                        pe.wait_ge(h_done, 2 * NF * i + e * NF + f + 1)
                        last = pe.matmul(ps_o, w2[par][:, e, f, :], HT[e][:, f, :],
                                         start=(f == 0), stop=(f == NF - 1))
                    last.then_inc(o_ps, 1)

                for c in range(NF):
                    inner(c)
                if not first:
                    rows_back(i - 1)
                for c in range(NF, 2 * NF - 1):
                    inner(c)
                outer(0)
                last = isinstance(i, int) and i == NPAIR - 1
                if not last:
                    xt(i + 1, 1 - par, k + par)
                inner(2 * NF - 1)
                if last:
                    part, n0, n1 = LAST_PARTS[0]
                    rows_back(part, 2 * NPAIR - 1, n0, n1)
                outer(1)
                if last:
                    part, n0, n1 = LAST_PARTS[1]
                    rows_back(part, 2 * NPAIR, n0, n1)

            xt(0, 0, 0)
            in_pairs(pe, experts)


_INS = ['L0_attn_x', 'L0_attn_w_qkv', 'L0_attn_w_swiglu', 'L0_attn_w_out', 'L0_ffn_gate_w', 'L0_ffn_w1',
        'L0_ffn_w2', 'L0_c', 'L0_wmod']
_OUTS = [((8, 512, 128), 'float32')]


def kernel(**inputs):
    import numpy as _np
    import concourse.bacc as _bacc
    from concourse import mybir as _mybir
    from concourse.bass_utils import run_bass_kernel_spmd as _run

    nc = _bacc.Bacc("TRN2", target_bir_lowering=False, num_devices=1)
    arrays, args = {}, []
    for name in _INS:
        a = _np.ascontiguousarray(inputs[name])
        arrays[f"in_{name}_dram"] = a
        args.append(nc.dram_tensor(f"in_{name}_dram", a.shape, _mybir.dt.from_np(a.dtype), kind="ExternalInput").ap())
    for i, (shape, dtype) in enumerate(_OUTS):
        dt = _mybir.dt.from_np(_np.dtype(dtype))
        args.append(nc.dram_tensor(f"out_{i}_dram", shape, dt, kind="ExternalOutput").ap())
    adaln_attention_moe(nc, *args)
    r = _run(nc, [arrays], core_ids=[0])
    got = tuple(r.results[0][f"out_{i}_dram"] for i in range(len(_OUTS)))
    return got[0]
```
